# Optimizing a Trainium2 kernel written in Bass

```python
import numpy as np
import jax
import jax.numpy as jnp

def _softmax(x, axis=-1):
    return jax.nn.softmax(x, axis=axis)

def _gelu(x):
    return jax.nn.gelu(x, approximate=True)

def _silu(x):
    return jax.nn.silu(x)

def _sigmoid(x):
    return jax.nn.sigmoid(x)

def _layernorm(x, axis=-1, eps=1e-05):
    m = jnp.mean(x, axis=axis, keepdims=True)
    v = jnp.var(x, axis=axis, keepdims=True)
    return (x - m) / jnp.sqrt(v + eps)

def _scatter_add(tgt, idx, src, axis=0):
    return tgt.at[idx].add(src)

def _segment_sum(src, seg, n):
    return jax.ops.segment_sum(src, seg, n)
kernel_name = 'mk_macaron_d1_jaxref_r8_d5aca3'

def setup_inputs(seed: int=0):
    np.random.seed(seed)
    _w = jnp.asarray

    def _L0_attn_setup():
        import jax, jax.numpy as jnp
        import numpy as np
        EMBED = 128
        HEADS = 16
        HDIM = EMBED // HEADS
        B, S = (4, 512)
        key = jax.random.key(seed)
        ks = jax.random.split(key, 11)
        scale = 1.0 / np.sqrt(EMBED)

        def lin(k):
            return jax.random.uniform(k, (EMBED, EMBED), jnp.float32, -scale, scale)

        def bias(k):
            return jax.random.uniform(k, (EMBED,), jnp.float32, -scale, scale)
        return {'x': jax.random.normal(ks[0], (B, S, EMBED), jnp.float32), 'Wq': lin(ks[1]), 'bq': bias(ks[2]), 'Wk': lin(ks[3]), 'bk': bias(ks[4]), 'Wv': lin(ks[5]), 'bv': bias(ks[6]), 'Wg': lin(ks[7]), 'bg': bias(ks[8]), 'Wo': lin(ks[9]), 'bo': bias(ks[10])}
    _L0_attn_in = _L0_attn_setup()

    def _L0_ffn_setup():
        import jax, jax.numpy as jnp
        import numpy as np
        B, T, D, F, E = (4, 256, 128, 512, 8)
        key = jax.random.key(seed)
        k = jax.random.split(key, 7)
        x = jax.random.normal(k[0], (B, T, D), dtype=jnp.float32)
        wr = jax.random.normal(k[1], (D,), dtype=jnp.float32)
        br = jnp.zeros((), dtype=jnp.float32)
        W1 = jax.random.normal(k[2], (E, D, F), dtype=jnp.float32) * 0.02
        b1 = jnp.zeros((E, F), dtype=jnp.float32)
        W2 = jax.random.normal(k[3], (E, F, D), dtype=jnp.float32) * 0.02
        b2 = jnp.zeros((E, D), dtype=jnp.float32)
        return {'x': x, 'wr': wr, 'br': br, 'W1': W1, 'b1': b1, 'W2': W2, 'b2': b2}
    _L0_ffn_in = _L0_ffn_setup()
    _d = {'L0_attn_x': _L0_attn_in['x'], 'L0_attn_Wq': _L0_attn_in['Wq'], 'L0_attn_bq': _L0_attn_in['bq'], 'L0_attn_Wk': _L0_attn_in['Wk'], 'L0_attn_bk': _L0_attn_in['bk'], 'L0_attn_Wv': _L0_attn_in['Wv'], 'L0_attn_bv': _L0_attn_in['bv'], 'L0_attn_Wg': _L0_attn_in['Wg'], 'L0_attn_bg': _L0_attn_in['bg'], 'L0_attn_Wo': _L0_attn_in['Wo'], 'L0_attn_bo': _L0_attn_in['bo'], 'L0_ffn_wr': _L0_ffn_in['wr'], 'L0_ffn_br': _L0_ffn_in['br'], 'L0_ffn_W1': _L0_ffn_in['W1'], 'L0_ffn_b1': _L0_ffn_in['b1'], 'L0_ffn_W2': _L0_ffn_in['W2'], 'L0_ffn_b2': _L0_ffn_in['b2']}
    _x0 = _d['L0_attn_x']
    _d['L0_attn_x'] = jax.random.normal(jax.random.fold_in(jax.random.key(seed), 1), (8, 256, 128), dtype=_x0.dtype)
    del _x0
    return _d

def reference(L0_attn_x, L0_attn_Wq, L0_attn_bq, L0_attn_Wk, L0_attn_bk, L0_attn_Wv, L0_attn_bv, L0_attn_Wg, L0_attn_bg, L0_attn_Wo, L0_attn_bo, L0_ffn_wr, L0_ffn_br, L0_ffn_W1, L0_ffn_b1, L0_ffn_W2, L0_ffn_b2):

    def _L0_attn_ref(x, Wq, bq, Wk, bk, Wv, bv, Wg, bg, Wo, bo):
        import jax, jax.numpy as jnp
        import numpy as np
        EMBED = 128
        HEADS = 16
        HDIM = EMBED // HEADS
        B, S = (4, 512)
        b, s, _ = x.shape

        def split_heads(t):
            return t.reshape(b, s, HEADS, HDIM).transpose(0, 2, 1, 3)
        q = split_heads(x @ Wq + bq)
        k = split_heads(x @ Wk + bk)
        v = split_heads(x @ Wv + bv)
        q = jax.nn.elu(q) + 1.0
        k = jax.nn.elu(k) + 1.0
        kv = jnp.einsum('bhsd,bhse->bhde', k, v)
        attn = jnp.einsum('bhsd,bhde->bhse', q, kv)
        attn = attn.transpose(0, 2, 1, 3).reshape(b, s, EMBED)
        gate = jax.nn.sigmoid(x @ Wg + bg)
        out = gate * attn @ Wo + bo
        return out

    def _L0_ffn_ref(x, wr, br, W1, b1, W2, b2):
        import jax, jax.numpy as jnp
        import numpy as np
        B, T, D, F, E = (4, 256, 128, 512, 8)
        keys = jnp.einsum('btd,d->bt', x, wr) + br
        expert_idx = jnp.mod(jnp.floor(keys).astype(jnp.int32), W1.shape[0])
        out = jnp.zeros_like(x)
        for e in range(W1.shape[0]):
            h = jax.nn.relu(jnp.einsum('btd,df->btf', x, W1[e]) + b1[e])
            y = jnp.einsum('btf,fd->btd', h, W2[e]) + b2[e]
            out = jnp.where((expert_idx == e)[..., None], y, out)
        return out
    x = L0_attn_x
    x = x + 0.5 * _L0_ffn_ref(_layernorm(x, axis=-1), L0_ffn_wr, L0_ffn_br, L0_ffn_W1, L0_ffn_b1, L0_ffn_W2, L0_ffn_b2)
    x = x + _L0_attn_ref(_layernorm(x, axis=-1), L0_attn_Wq, L0_attn_bq, L0_attn_Wk, L0_attn_bk, L0_attn_Wv, L0_attn_bv, L0_attn_Wg, L0_attn_bg, L0_attn_Wo, L0_attn_bo)
    x = x + 0.5 * _L0_ffn_ref(_layernorm(x, axis=-1), L0_ffn_wr, L0_ffn_br, L0_ffn_W1, L0_ffn_b1, L0_ffn_W2, L0_ffn_b2)
    return x

_drawn_inputs = setup_inputs


def setup_inputs(seed=0):
    import zlib

    import numpy as np

    out = dict(_drawn_inputs(seed))
    spreads = {'L0_ffn_b1': (0.0, 0.1), 'L0_ffn_b2': (0.0, 0.1)}
    factors = {'L0_attn_bq': 4.332, 'L0_attn_bk': 3.913, 'L0_attn_bo': 47.369, 'L0_ffn_W1': 2.799}
    for name, (base, spread) in spreads.items():
        noise = np.random.default_rng([zlib.crc32(name.encode()), seed]).standard_normal(out[name].shape)
        drawn = base * np.exp(spread * noise) if base else spread * noise
        out[name] = jnp.asarray(drawn.astype(out[name].dtype))
    for name, factor in factors.items():
        out[name] = (out[name] * factor).astype(out[name].dtype)
    return out
```

```python
from contextlib import ExitStack

import numpy as np
import concourse.bass as bass
from concourse import mybir

FP32, FP16, BF16 = mybir.dt.float32, mybir.dt.float16, mybir.dt.bfloat16
I32, U32 = mybir.dt.int32, mybir.dt.uint32
ALU = mybir.AluOpType
ACT = mybir.ActivationFunctionType
AX = mybir.AxisListType

P = 128
B, S, D = 8, 256, 128
E, F = 8, 512
TOKENS = B * S
TT = TOKENS // P
FC = F // P
NT = TT + E - 1
PER_BATCH = S // P
HEAD = 8
EPS = 1e-5

RES, ID, ROW = D, 2 * D, 2 * D + 4
ID_BASE = 4096
NSCALE = 4096.0
WTOP = 2.0 ** 14
HSCALE = 2.0 ** -19
HUNIT = HSCALE * NSCALE


def build(nc, x_d, wq_d, bq_d, wk_d, bk_d, wv_d, bv_d, wg_d, bg_d, wo_d, bo_d,
          wr_d, br_d, w1_d, b1_d, w2_d, b2_d, out_d, sorted_d, mid_d):
    ctx = ExitStack()
    with ctx:
        def sb(name, shape, dt=FP32):
            return ctx.enter_context(nc.sbuf_tensor(name, shape, dt))

        def ps(name, shape, dt=FP32):
            return ctx.enter_context(nc.psum_tensor(name, shape, dt))

        def sem(name):
            return ctx.enter_context(nc.semaphore(name))

        rows = sb("rows", [P, TT, ROW])
        rows16 = rows[:].rearrange("p t w -> p (t w)").bitcast(FP16).rearrange("p (t w) -> p t w", t=TT)
        norm = sb("norm", [P, TT, D])
        x1 = sb("x1", [P, TT, D])
        x1bo = sb("x1bo", [P, TT, D])
        w1 = sb("w1", [P, E, F])
        w2 = sb("w2", [P, E, FC, D])
        w1h, w1l = sb("w1h", [P, E, F], FP16), sb("w1l", [P, E, F], FP16)
        w2h, w2l = sb("w2h", [P, E, FC, D], FP16), sb("w2l", [P, E, FC, D], FP16)
        b1raw = sb("b1raw", [E * FC, P])
        b1t = sb("b1t", [P, E, FC])
        b2b = sb("b2b", [P, E, D])
        wa = sb("wa", [P, 4, D])
        wah, wal = sb("wah", [P, 4, D], FP16), sb("wal", [P, 4, D], FP16)
        wo = sb("wo", [P, D])
        bqg = sb("bqg", [P, 2])
        bkv = sb("bkv", [P, 2, D])
        bob = sb("bob", [P, D])
        wrb = sb("wrb", [P, D])
        brb = sb("brb", [P, 1])
        ident16, ident32 = sb("ident16", [P, P], FP16), sb("ident32", [P, P])
        before = sb("before", [P, P], BF16)
        ones = sb("ones", [P, P], BF16)
        headmask = sb("headmask", [P, P])
        expert_no = sb("expert_no", [P, E, TT])
        tile_no = sb("tile_no", [P, NT, E])
        ones8 = sb("ones8", [P, P])
        minus_half, minus_one = sb("minus_half", [P, TT]), sb("minus_one", [P, 1])
        zero_row = sb("zero_row", [P, ROW])
        stats = sb("stats", [P, TT, 6])
        mv = sb("mv", [P, TT, 2])
        var = sb("var", [P, TT])
        rs0, rs1, rstd = sb("rs0", [P, TT]), sb("rs1", [P, TT]), sb("rstd", [P, TT])
        keyprod = sb("keyprod", [P, D])
        key = sb("key", [P, TT])
        rk, rki, rkf = sb("rk", [P, TT]), sb("rki", [P, TT], I32), sb("rkf", [P, TT])
        rgt = sb("rgt", [P, TT])
        onehot = sb("onehot", [P, E, TT], BF16)
        tot = sb("tot", [P, E, TT])
        cum = sb("cum", [P, E, TT])
        cnt = sb("cnt", [P, E])
        cnti, nti = sb("cnti", [P, E], I32), sb("nti", [P, E], I32)
        ntf = sb("ntf", [P, E])
        endt = sb("endt", [P, E])
        scan = sb("scan", [P, E, TT])
        adj = sb("adj", [P, E])
        base = sb("base", [P, E, TT])
        posf = sb("posf", [P, TT])
        pos = sb("pos", [P, TT], I32)
        past = sb("past", [P, NT, E])
        tef = sb("tef", [P, NT])
        te = [sb(f"te{f}", [P, NT + 4], I32) for f in range(2)]
        wmax = sb("wmax", [P, 4])
        gmax = sb("gmax", [P, 4])
        sexp, sinv, sup = sb("sexp", [P, 4]), sb("sinv", [P, 4]), sb("sup", [P, 4])
        cy, ca, cg = sb("cy", [P, 1]), sb("ca", [P, 1]), sb("cg", [P, 1])
        s1h = sb("s1h", [P, 1])
        xin = sb("xin", [P, 4, ROW])
        xin16 = xin[:].rearrange("p t w -> p (t w)").bitcast(FP16).rearrange("p (t w) -> p t w", t=4)
        xini = xin[:].rearrange("p t w -> p (t w)").bitcast(I32).rearrange("p (t w) -> p t w", t=4)
        xt = sb("xt", [P, 2, 2, P], FP16)
        h32 = sb("h32", [P, 2, FC, P])
        hh, hl = sb("hh", [P, 2, FC, P], FP16), sb("hl", [P, 2, FC, P], FP16)
        yb = sb("yb", [P, 4, D])
        yout = sb("yout", [P, 4, D])
        sidx = sb("sidx", [P, 4], I32)
        nt_sb = sb("nt_sb", [P, 2, 2, S], FP16)
        q1, qe, qt = sb("q1", [P, 2, S]), sb("qe", [P, 2, S]), sb("qt", [P, 2, S])
        gt = sb("gt", [P, 2, S])
        nh2, nl2 = sb("nh2", [P, 2, PER_BATCH, D], FP16), sb("nl2", [P, 2, PER_BATCH, D], FP16)
        kv1 = sb("kv1", [P, 2, PER_BATCH, 2, D])
        ke = sb("ke", [P, 2, PER_BATCH, D])
        kk = sb("kk", [P, 2, PER_BATCH, D])
        kvm = sb("kvm", [P, 2, P])
        gat = sb("gat", [P, 2, S])

        bank = [ps(f"bank{i}", [P, 512]) for i in range(8)]
        xt_ps = [bank[i][:, 0:P].bitcast(FP16).rearrange("p (a n) -> p a n", a=2) for i in (0, 1)]
        h_ps = [bank[i][:].rearrange("p (c n) -> p c n", c=FC) for i in (2, 3)]
        y_ps = [bank[i][:, 0:D] for i in (4, 5)]
        r_ps = bank[6][:, 0:2 * P].rearrange("p (a e t) -> p a e t", a=2, e=E)
        b1_ps = bank[7][:, 0:E * FC]
        nt_ps = bank[0][:, 0:S].bitcast(FP16).rearrange("p (a n) -> p a n", a=2)
        q_ps, g_ps = bank[1][:, 0:S], bank[7][:, 0:S]
        kv_ps = bank[2][:].rearrange("p (t a n) -> p t a n", t=PER_BATCH, a=2)
        kvh_ps = bank[3][:, 0:P]
        at_ps = bank[4][:, 0:S]
        o_ps = bank[5][:, 0:S].rearrange("p (t n) -> p t n", t=PER_BATCH)

        x_in = [sem(f"x_in{i}") for i in range(4)]
        small_in, w1_in, w2_in, wa_in, zeroed = sem("small_in"), sem("w1_in"), sem("w2_in"), sem("wa_in"), [sem(f"zeroed{f}") for f in range(2)]
        consts_done = sem("consts_done")
        dve_step, act_step, pool_step = sem("dve_step"), sem("act_step"), sem("pool_step")
        b1_turned, maxes, maxed, scales = sem("b1_turned"), sem("maxes"), sem("maxed"), sem("scales")
        w_high, w_low = sem("w_high"), sem("w_low")
        var_ready, pow_ready = sem("var_ready"), sem("pow_ready")
        norm_ready, row_high, row_low = sem("norm_ready"), sem("row_high"), sem("row_low")
        onehot_ready, ranked = sem("onehot_ready"), sem("ranked")
        routed = sem("routed")
        L = []
        for f in range(2):
            L.append({n: sem(f"f{f}_{n}") for n in
                      ("dispatched", "xt_done", "xt_copied", "h_done", "relu_done", "hh_done", "hl_done",
                       "y_done", "y_evac", "idx_done", "res_added")}
                     | {"xin": [sem(f"f{f}_xin{u}") for u in range(4)],
                        "stored": [sem(f"f{f}_stored{u}") for u in range(4)]})
        x1_in = [sem(f"x1_in{i}") for i in range(4)]
        x1bo_ready = sem("x1bo_ready")
        nt_done, nt_copied = sem("nt_done"), sem("nt_copied")
        q_done, g_done, kv_done = sem("q_done"), sem("g_done"), sem("kv_done")
        n2_high, n2_low = sem("n2_high"), sem("n2_low")
        q1_ready, qe_ready, q_ready, g_ready = sem("q1_ready"), sem("qe_ready"), sem("q_ready"), sem("g_ready")
        kv1_ready, ke_ready, k_ready = sem("kv1_ready"), sem("ke_ready"), sem("k_ready")
        kvh_done, kvm_ready, at_done, gated_ready = sem("kvh_done"), sem("kvm_ready"), sem("at_done"), sem("gated_ready")
        o_done, x2_ready = sem("o_done"), sem("x2_ready")

        block = ctx.enter_context(nc.Block())

        x_v = x_d.rearrange("b (h p) d -> p (b h) d", p=P)
        mid_v = mid_d.rearrange("(t p) d -> p t d", p=P)
        out_rows = out_d.rearrange("b s d -> (b s) d")

        @block.sync
        def _(sp):
            for i in range(4):
                sp.dma_start(rows[:, 4 * i:4 * i + 4, RES:RES + D], x_v[:, 4 * i:4 * i + 4, :]).then_inc(x_in[i], 16)
            sp.dma_start(wrb[:], wr_d.rearrange("(a n) -> a n", a=1).to_broadcast([P, D])).then_inc(small_in, 16)
            sp.dma_start(brb[:], br_d.to_broadcast([P, 1])).then_inc(small_in, 16)
            sp.dma_start(b1raw[:], b1_d.rearrange("e (c p) -> (e c) p", p=P)).then_inc(small_in, 16)
            sp.dma_start(b2b[:].rearrange("p e d -> p (e d)"),
                         b2_d.rearrange("(a e) d -> a (e d)", a=1).to_broadcast([P, E * D])).then_inc(small_in, 16)
            for q in range(4):
                sp.dma_start(w1[:, 2 * q:2 * q + 2, :],
                             w1_d[2 * q:2 * q + 2].rearrange("e p f -> p e f")).then_inc(w1_in, 16)
            for q in range(4):
                sp.dma_start(w2[:, 2 * q:2 * q + 2], w2_d[2 * q:2 * q + 2].rearrange("e (c p) d -> p e c d", p=P)).then_inc(w2_in, 16)
            for i, w in enumerate((wq_d, wg_d, wk_d, wv_d)):
                sp.dma_start(wa[:, i, :], w).then_inc(wa_in, 16)
            sp.dma_start(wo[:], wo_d).then_inc(wa_in, 16)
            for i, b in enumerate((bq_d, bg_d)):
                sp.dma_start(bqg[:, i:i + 1], b.rearrange("(n a) -> n a", a=1)).then_inc(wa_in, 16)
            for i, b in enumerate((bk_d, bv_d)):
                sp.dma_start(bkv[:, i, :], b.rearrange("(a n) -> a n", a=1).to_broadcast([P, D])).then_inc(wa_in, 16)
            sp.dma_start(bob[:], bo_d.rearrange("(a n) -> a n", a=1).to_broadcast([P, D])).then_inc(wa_in, 16)

            def load_tiles(f):
                s, src = L[f], sorted_d[f]
                sp.wait_ge(s["dispatched"], 16 * TT)

                def load(t, u):
                    if not isinstance(t, int) or t >= 4:
                        sp.wait_ge(s["xt_done"], t - 3)
                        sp.wait_ge(s["res_added"], t - 3)
                    sp.dma_start(xin[:, u, :], src[bass.ds(t * P, P), :]).then_inc(s["xin"][u], 16)
                for t in range(4):
                    load(t, t)
                with sp.Fori(4, 20, 4) as t:
                    for u in range(4):
                        load(t + u, u)
                for t in range(20, NT):
                    load(t, t % 4)

            load_tiles(0)
            for u in range(4):
                sp.wait_ge(L[0]["stored"][u], 16 * len(range(u, NT, 4)))
            for i in range(4):
                sp.dma_start(x1[:, 4 * i:4 * i + 4, :], mid_v[:, 4 * i:4 * i + 4, :]).then_inc(x1_in[i], 16)
            load_tiles(1)
            for u in range(4):
                sp.wait_ge(L[1]["stored"][u], 16 * len(range(u, NT, 4)))

        TURNS = B + 3

        def rsqrt_number(kind, b):
            if kind == "x":
                return b + 1
            asked = B
            for i in range(TURNS):
                for k, c in (("attn", i), ("ffn", i - 3)):
                    if 0 <= c < B:
                        asked += 1
                        if (k, c) == (kind, b):
                            return asked

        @block.gpsimd
        def _(pool):
            n = [0]

            def step(ins):
                n[0] += 1
                ins.then_inc(pool_step, 1)
                pool.wait_ge(pool_step, n[0])

            def fill(f):
                pool.dma_start(sorted_d[f].rearrange("(p k) w -> p k w", p=P),
                               zero_row[:].rearrange("p (a w) -> p a w", a=1).to_broadcast([P, NT, ROW])
                               ).then_inc(zeroed[f], 16)

            step(nc.gpsimd.memset(zero_row[:], 0.0))
            fill(0)
            nc.gpsimd.memset(minus_half[:], -0.5)
            nc.gpsimd.memset(ident16[:], 0.0)
            nc.gpsimd.memset(ident32[:], 0.0)
            nc.gpsimd.memset(ones[:], 1.0)
            nc.gpsimd.memset(ones8[:], 1.0)
            nc.gpsimd.memset(before[:], 0.0)
            nc.gpsimd.memset(rows[:, :, ID + 1:ROW], 0.0)
            step(nc.gpsimd.memset(headmask[:], 1.0))
            nc.gpsimd.iota(rows[:].bitcast(I32)[:, :, ID:ID + 1], pattern=[[-P, TT]], base=ID_BASE,
                           channel_multiplier=-1)
            nc.gpsimd.iota(expert_no[:], pattern=[[1, E], [0, TT]], base=0, channel_multiplier=0,
                           allow_small_or_imprecise_dtypes=True)
            nc.gpsimd.iota(tile_no[:], pattern=[[1, NT], [0, E]], base=0, channel_multiplier=0,
                           allow_small_or_imprecise_dtypes=True)
            for m in (ident16, ident32):
                nc.gpsimd.affine_select(out=m[:], in_=m[:], compare_op=ALU.not_equal, fill=1.0, base=0,
                                        pattern=[[-1, P]], channel_multiplier=1)
            nc.gpsimd.affine_select(out=before[:], in_=before[:], compare_op=ALU.is_ge, fill=1.0, base=0,
                                    pattern=[[-1, P]], channel_multiplier=1)
            hm = headmask[:].rearrange("p (g n) -> p g n", n=HEAD)
            step(nc.gpsimd.affine_select(out=hm, in_=hm, compare_op=ALU.is_ge, fill=0.0, base=0,
                                         pattern=[[-HEAD, P // HEAD], [0, HEAD]], channel_multiplier=1))
            nc.gpsimd.affine_select(out=hm, in_=hm, compare_op=ALU.is_ge, fill=0.0, base=HEAD - 1,
                                    pattern=[[HEAD, P // HEAD], [0, HEAD]], channel_multiplier=-1
                                    ).then_inc(consts_done, 1)

            def rsqrt_guess(kind, b):
                pool.wait_ge(var_ready, rsqrt_number(kind, b))
                v = slice(2 * b, 2 * b + 2)
                nc.gpsimd.tensor_tensor(rs0[:, v], var[:, v], minus_half[:, v], ALU.pow).then_inc(pow_ready, 1)

            def row_lows(f, b):
                pool.wait_ge(row_high, B * f + b + 1)
                v = slice(2 * b, 2 * b + 2)
                nc.gpsimd.tensor_tensor(rows16[:, v, D:2 * D], norm[:, v, :], rows16[:, v, 0:D],
                                        ALU.subtract).then_inc(row_low, 1)

            def dispatch(f):
                pool.wait_ge(zeroed[f], 16)
                pool.wait_ge(routed, f + 1)
                pool.wait_ge(row_low, (f + 1) * B)
                for j in range(TT):
                    nc.gpsimd.indirect_dma_start(
                        sorted_d[f], bass.IndirectOffsetOnAxis(ap=pos[:, j:j + 1].bitcast(U32), axis=0),
                        rows[:, j, :], None).then_inc(L[f]["dispatched"], 16)

            def combine(f):
                s = L[f]
                dst = (mid_d, out_rows)[f]
                for t in range(NT):
                    u = t % 4
                    pool.wait_ge(s["y_evac"], t + 1)
                    if t >= 4:
                        pool.wait_ge(s["stored"][u], 16 * (t // 4))
                    nc.gpsimd.tensor_tensor(yout[:, u, :], yb[:, u, :], xin[:, u, RES:RES + D],
                                            ALU.add).then_inc(s["res_added"], 1)
                    pool.wait_ge(s["res_added"], t + 1)
                    nc.gpsimd.indirect_dma_start(
                        dst, bass.IndirectOffsetOnAxis(ap=sidx[:, u:u + 1].bitcast(U32), axis=0),
                        yout[:, u, :], None, bounds_check=TOKENS - 1, oob_is_err=False
                    ).then_inc(s["stored"][u], 16)

            for b in range(B):
                rsqrt_guess("x", b)
            for b in range(B):
                row_lows(0, b)
            dispatch(0)
            pool.wait_ge(maxes, 4)
            nc.gpsimd.partition_all_reduce(gmax[:], wmax[:], P, bass.bass_isa.ReduceOp.max).then_inc(maxed, 1)
            fill(1)
            combine(0)
            for b in range(B):
                v = slice(2 * b, 2 * b + 2)
                if b % 2 == 0:
                    pool.wait_ge(x1_in[b // 2], 16)
                if b == 0:
                    pool.wait_ge(wa_in, 16 * 10)
                nc.gpsimd.tensor_tensor(x1bo[:, v, :], x1[:, v, :],
                                        bob[:].rearrange("p (a n) -> p a n", a=1).to_broadcast([P, 2, D]),
                                        ALU.add).then_inc(x1bo_ready, 1)
            for i in range(TURNS):
                if i < B:
                    rsqrt_guess("attn", i)
                if i >= 3:
                    rsqrt_guess("ffn", i - 3)
                if i < B:
                    pool.wait_ge(n2_high, i + 1)
                    if i >= 2:
                        pool.wait_ge(nt_done, i - 1)
                    nc.gpsimd.tensor_tensor(nl2[:, i % 2], norm[:, 2 * i:2 * i + 2, :], nh2[:, i % 2],
                                            ALU.subtract).then_inc(n2_low, 1)
                if i >= 3:
                    row_lows(1, i - 3)
            dispatch(1)
            combine(1)

        @block.scalar
        def _(act):
            def row_highs(f, b, number):
                act.wait_ge(norm_ready, number)
                v = slice(2 * b, 2 * b + 2)
                nc.scalar.activation(rows16[:, v, 0:D], norm[:, v, :], ACT.Copy).then_inc(row_high, 1)

            for b in range(B):
                row_highs(0, b, b + 1)
            act.wait_ge(scales, 1)
            for e in range(0, E, 2):
                nc.scalar.activation(w1h[:, e:e + 2], w1[:, e:e + 2], ACT.Copy, scale=sup[:, 0:1]).then_inc(w_high, 1)
            for e in range(0, E, 2):
                nc.scalar.activation(w2h[:, e:e + 2], w2[:, e:e + 2], ACT.Copy, scale=sup[:, 1:2]).then_inc(w_high, 1)
            nc.scalar.activation(wah[:], wa[:], ACT.Copy, scale=sup[:, 2:3]).then_inc(w_high, 1)

            def ffn(f):
                s = L[f]
                act.wait_ge(routed, f + 1)

                def hidden(t, k):
                    e = act.value_load(te[f][0:1, bass.ds(t, 1)], min_val=0, max_val=E - 1)
                    act.wait_ge(s["h_done"], t + 1)
                    if not isinstance(t, int) or t >= 2:
                        act.wait_ge(s["hl_done"], t - 1)
                    for c in range(FC):
                        ins = nc.scalar.activation(h32[:, k, c, :], h_ps[k][:, c, :], ACT.Relu,
                                                   bias=b1t[:, bass.ds(e, 1), c:c + 1].rearrange("p a b -> p (a b)"),
                                                   scale=HSCALE)
                    ins.then_inc(s["relu_done"], 1)
                for t in range(4):
                    hidden(t, t % 2)
                with act.Fori(4, 20, 4) as t:
                    for u in range(4):
                        hidden(t + u, u % 2)
                for t in range(20, NT):
                    hidden(t, t % 2)

            ffn(0)
            for i in range(TURNS):
                b = i - 1
                if 0 <= b < B:
                    k = b % 2
                    act.wait_ge(q1_ready, b + 1)
                    nc.scalar.activation(qe[:, k], q1[:, k], ACT.Exp, bias=minus_one[:, 0:1]).then_inc(qe_ready, 1)
                    act.wait_ge(g_done, b + 1)
                    if b >= 2:
                        act.wait_ge(gated_ready, b - 1)
                    nc.scalar.activation(gt[:, k], g_ps, ACT.Tanh, bias=bqg[:, 1:2], scale=cg[:, 0:1]).then_inc(g_ready, 1)
                    act.wait_ge(kv1_ready, b + 1)
                    nc.scalar.activation(ke[:, k], kv1[:, k, :, 0, :], ACT.Exp, bias=minus_one[:, 0:1]).then_inc(ke_ready, 1)
                if i < B:
                    k = i % 2
                    act.wait_ge(norm_ready, rsqrt_number("attn", i))
                    if i >= 2:
                        act.wait_ge(nt_done, i - 1)
                    nc.scalar.activation(nh2[:, k], norm[:, 2 * i:2 * i + 2, :], ACT.Copy).then_inc(n2_high, 1)
                    act.wait_ge(nt_done, i + 1)
                    if i >= 2:
                        act.wait_ge(kv_done, i - 1)
                    nc.scalar.activation(nt_sb[:, k], nt_ps, ACT.Copy).then_inc(nt_copied, 1)
                if i >= 3:
                    row_highs(1, i - 3, rsqrt_number("ffn", i - 3))
            ffn(1)

        @block.tensor
        def _(pe):
            def split_matmul(out, whi, wlo, xhi, xlo):
                nc.tensor.matmul(out, whi, xhi, start=True, stop=False)
                nc.tensor.matmul(out, whi, xlo, start=False, stop=False)
                return nc.tensor.matmul(out, wlo, xhi, start=False, stop=True)

            pe.wait_ge(consts_done, 1)
            pe.wait_ge(small_in, 16 * 4)
            nc.tensor.transpose(b1_ps, b1raw[:], ident32[0:E * FC, 0:E * FC]).then_inc(b1_turned, 1)

            def rank(f):
                pe.wait_ge(onehot_ready, f + 1)
                oh = onehot[:].rearrange("p e t -> p (e t)")
                nc.tensor.matmul(r_ps[:, 0].rearrange("p e t -> p (e t)"), before[:], oh, start=True, stop=True)
                nc.tensor.matmul(r_ps[:, 1].rearrange("p e t -> p (e t)"), ones[:], oh,
                                 start=True, stop=True).then_inc(ranked, 1)

            def ffn(f):
                s = L[f]

                def turn(t, u):
                    k = u % 2
                    pe.wait_ge(s["xin"][u], 16 * (t // 4 + 1) if isinstance(t, int) else 4 * (t - u) + 16)
                    if not isinstance(t, int) or t >= 2:
                        pe.wait_ge(s["xt_copied"], t - 1)
                    for a in range(2):
                        ins = nc.tensor.transpose(xt_ps[k][:, a, :], xin16[:, u, a * D:(a + 1) * D], ident16[:])
                    ins.then_inc(s["xt_done"], 1)

                def first(t, u, e):
                    k = u % 2
                    pe.wait_ge(s["xt_copied"], t + 1)
                    if not isinstance(t, int) or t >= 2:
                        pe.wait_ge(s["relu_done"], t - 1)
                    for c in range(FC):
                        cols = slice(c * P, (c + 1) * P)
                        ins = split_matmul(h_ps[k][:, c, :],
                                           w1h[:, bass.ds(e, 1), cols].rearrange("p a n -> p (a n)"),
                                           w1l[:, bass.ds(e, 1), cols].rearrange("p a n -> p (a n)"),
                                           xt[:, k, 0, :], xt[:, k, 1, :])
                    ins.then_inc(s["h_done"], 1)

                def second(t, u, e):
                    k = u % 2
                    pe.wait_ge(s["hl_done"], t + 1)
                    if not isinstance(t, int) or t >= 2:
                        pe.wait_ge(s["y_evac"], t - 1)
                    for c in range(FC):
                        wh = w2h[:, bass.ds(e, 1), c, :].rearrange("p a n -> p (a n)")
                        wl = w2l[:, bass.ds(e, 1), c, :].rearrange("p a n -> p (a n)")
                        nc.tensor.matmul(y_ps[k], hh[:, k, c, :], wh, start=(c == 0), stop=False)
                        nc.tensor.matmul(y_ps[k], hh[:, k, c, :], wl, start=False, stop=False)
                        ins = nc.tensor.matmul(y_ps[k], hl[:, k, c, :], wh, start=False, stop=(c == FC - 1))
                    ins.then_inc(s["y_done"], 1)

                def expert(t):
                    return pe.value_load(te[f][0:1, bass.ds(t, 1)], min_val=0, max_val=E - 1)

                pe.wait_ge(routed, f + 1)
                pe.wait_ge(w_low, 9)
                e = expert(0)
                turn(0, 0)
                first(0, 0, e)
                turn(1, 1)

                def tile(t, u, e):
                    if not isinstance(t, int) or t + 1 < NT:
                        e_next = expert(t + 1)
                        first(t + 1, (u + 1) % 4, e_next)
                    if not isinstance(t, int) or t + 2 < NT:
                        turn(t + 2, (u + 2) % 4)
                    second(t, u, e)

                for t in range(4):
                    tile(t, t, expert(t))
                with pe.Fori(4, 20, 4) as t:
                    for u in range(4):
                        tile(t + u, u, expert(t + u))
                for t in range(20, NT):
                    tile(t, t % 4, expert(t))

            rank(0)
            ffn(0)
            for i in range(TURNS):
                c = i - 2
                if 0 <= c < B:
                    k = c % 2
                    pe.wait_ge(k_ready, c + 1)
                    if c >= 1:
                        pe.wait_ge(kvm_ready, c)
                    for j in range(PER_BATCH):
                        ins = nc.tensor.matmul(kvh_ps, kk[:, k, j, :], kv1[:, k, j, 1, :],
                                               start=(j == 0), stop=(j == PER_BATCH - 1))
                    ins.then_inc(kvh_done, 1)
                    pe.wait_ge(kvm_ready, c + 1)
                    pe.wait_ge(q_ready, c + 1)
                    if c >= 1:
                        pe.wait_ge(gated_ready, c)
                    nc.tensor.matmul(at_ps, kvm[:, k], qt[:, k], start=True, stop=True).then_inc(at_done, 1)
                if i < B:
                    k = i % 2
                    pe.wait_ge(n2_high, i + 1)
                    pe.wait_ge(n2_low, i + 1)
                    if i >= 1:
                        pe.wait_ge(nt_copied, i)
                    for j in range(PER_BATCH):
                        for a, src in enumerate((nh2, nl2)):
                            ins = nc.tensor.transpose(nt_ps[:, a, j * P:(j + 1) * P], src[:, k, j, :], ident16[:])
                    ins.then_inc(nt_done, 1)
                if 0 <= c < B:
                    k = c % 2
                    pe.wait_ge(gated_ready, c + 1)
                    if c >= 1:
                        pe.wait_ge(x2_ready, c)
                    for j in range(PER_BATCH):
                        ins = nc.tensor.matmul(o_ps[:, j, :], gat[:, k, j * P:(j + 1) * P], wo[:],
                                               start=True, stop=True)
                    ins.then_inc(o_done, 1)
                if i < B:
                    k = i % 2
                    pe.wait_ge(nt_copied, i + 1)
                    if i >= 1:
                        pe.wait_ge(q1_ready, i)
                        pe.wait_ge(g_ready, i)
                    split_matmul(q_ps, wah[:, 0, :], wal[:, 0, :], nt_sb[:, k, 0, :], nt_sb[:, k, 1, :]).then_inc(q_done, 1)
                    split_matmul(g_ps, wah[:, 1, :], wal[:, 1, :], nt_sb[:, k, 0, :], nt_sb[:, k, 1, :]).then_inc(g_done, 1)
                    if i >= 1:
                        pe.wait_ge(kv1_ready, i)
                    kvh, kvl = (w[:, 2:4, :].rearrange("p a n -> p (a n)") for w in (wah, wal))
                    for j in range(PER_BATCH):
                        out = kv_ps[:, j].rearrange("p a n -> p (a n)")
                        th, tl = (nt_sb[:, k, a, j * P:(j + 1) * P] for a in range(2))
                        nc.tensor.matmul(out, th, kvh, start=True, stop=False)
                        nc.tensor.matmul(out, th, kvl, start=False, stop=False)
                        ins = nc.tensor.matmul(out, tl, kvh, start=False, stop=True)
                    ins.then_inc(kv_done, 1)
            rank(1)
            ffn(1)

        @block.vector
        def _(dve):
            n = [0]
            V = nc.vector

            def step(ins):
                n[0] += 1
                ins.then_inc(dve_step, 1)
                dve.wait_ge(dve_step, n[0])

            def variance(src, b):
                for j in (2 * b, 2 * b + 1):
                    ins = V.bn_stats(stats[:, j, :], src[:, j - 2 * b, :])
                step(ins)
                for j in (2 * b, 2 * b + 1):
                    ins = V.bn_aggr(mv[:, j, :], stats[:, j, :])
                step(ins)
                V.tensor_scalar(var[:, 2 * b:2 * b + 2], mv[:, 2 * b:2 * b + 2, 1], EPS, None, ALU.add
                                ).then_inc(var_ready, 1)

            def normalise(src, b, kind):
                dve.wait_ge(pow_ready, rsqrt_number(kind, b))
                v = slice(2 * b, 2 * b + 2)
                step(V.tensor_tensor(rs1[:, v], rs0[:, v], rs0[:, v], ALU.mult))
                step(V.tensor_tensor(rs1[:, v], rs1[:, v], var[:, v], ALU.mult))
                step(V.tensor_scalar(rs1[:, v], rs1[:, v], -0.5 * NSCALE, 1.5 * NSCALE, ALU.mult, ALU.add))
                step(V.tensor_tensor(rstd[:, v], rs1[:, v], rs0[:, v], ALU.mult))
                for j in (2 * b, 2 * b + 1):
                    ins = V.tensor_scalar(norm[:, j, :], src[:, j - 2 * b, :], mv[:, j, 0:1], rstd[:, j:j + 1],
                                          ALU.subtract, ALU.mult)
                ins.then_inc(norm_ready, 1)

            def keys(b, number):
                dve.wait_ge(norm_ready, number)
                for j in (2 * b, 2 * b + 1):
                    step(V.tensor_tensor_reduce(out=keyprod[:], in0=norm[:, j, :], in1=wrb[:], scale=1.0, scalar=0.0,
                                                op0=ALU.mult, op1=ALU.add, accum_out=key[:, j:j + 1]))

            def route(f):
                step(V.tensor_scalar(rk[:], key[:], 1.0 / NSCALE, brb[:, 0:1], ALU.mult, ALU.add))
                step(V.tensor_copy(rki[:], rk[:]))
                step(V.tensor_copy(rkf[:], rki[:]))
                step(V.tensor_tensor(rgt[:], rkf[:], rk[:], ALU.is_gt))
                step(V.tensor_tensor(rki[:], rkf[:], rgt[:], ALU.subtract))
                step(V.tensor_scalar(rki[:], rki[:], E - 1, None, ALU.bitwise_and))
                V.tensor_tensor(onehot[:], rki[:].rearrange("p (a t) -> p a t", a=1).to_broadcast([P, E, TT]),
                                expert_no[:], ALU.is_equal).then_inc(onehot_ready, 1)
                dve.wait_ge(ranked, f + 1)
                flat = lambda a: a[:].rearrange("p e t -> p (e t)")
                step(V.tensor_copy(tot[:], r_ps[:, 1]))
                V.tensor_reduce(cnt[:], tot[:], AX.X, ALU.add)
                step(V.tensor_tensor_scan(flat(scan), ones8[:], flat(tot), 0.0, ALU.mult, ALU.add))
                step(V.tensor_scalar(cnti[:], cnt[:], float(P - 1), None, ALU.add))
                V.tensor_tensor(scan[:], scan[:], tot[:], ALU.subtract)
                step(V.tensor_scalar(nti[:], cnti[:], 7, None, ALU.logical_shift_right))
                step(V.tensor_copy(ntf[:], nti[:]))
                step(V.tensor_tensor_scan(endt[:], ones8[:, 0:E], ntf[:], 0.0, ALU.mult, ALU.add))
                V.tensor_tensor(past[:], tile_no[:], endt[:].rearrange("p (a e) -> p a e", a=1).to_broadcast([P, NT, E]),
                                ALU.is_ge)
                step(V.tensor_tensor(adj[:], endt[:], ntf[:], ALU.subtract))
                V.tensor_reduce(tef[:], past[:], AX.X, ALU.add)
                step(V.scalar_tensor_tensor(adj[:], adj[:], float(P), scan[:, :, 0], ALU.mult, ALU.subtract))
                V.tensor_scalar(te[f][:, 0:NT], tef[:], float(E - 1), None, ALU.min)
                step(V.tensor_tensor(base[:], r_ps[:, 0], scan[:], ALU.add))
                step(V.tensor_tensor(base[:], base[:], adj[:].rearrange("p (e a) -> p e a", a=1).to_broadcast([P, E, TT]),
                                     ALU.add))
                step(V.tensor_tensor(base[:], base[:], onehot[:], ALU.mult))
                step(V.tensor_reduce(posf[:], base[:].rearrange("p e t -> p t e"), AX.X, ALU.add))
                V.tensor_copy(pos[:], posf[:]).then_inc(routed, 1)

            def ffn(f):
                s = L[f]

                def split_hidden(t, k):
                    dve.wait_ge(s["relu_done"], t + 1)
                    if not isinstance(t, int) or t >= 2:
                        dve.wait_ge(s["y_done"], t - 1)
                    V.tensor_copy(hh[:, k], h32[:, k]).then_inc(s["hh_done"], 1)
                    dve.wait_ge(s["hh_done"], t + 1)
                    V.tensor_tensor(hl[:, k], h32[:, k], hh[:, k], ALU.subtract).then_inc(s["hl_done"], 1)

                def copy_turned(t, k):
                    dve.wait_ge(s["xt_done"], t + 1)
                    if not isinstance(t, int) or t >= 2:
                        dve.wait_ge(s["h_done"], t - 1)
                    V.tensor_copy(xt[:, k], xt_ps[k]).then_inc(s["xt_copied"], 1)

                def output(t, u):
                    e = dve.value_load(te[f][0:1, bass.ds(t, 1)], min_val=0, max_val=E - 1)
                    dve.wait_ge(s["y_done"], t + 1)
                    if not isinstance(t, int) or t >= 4:
                        dve.wait_ge(s["stored"][u], 16 * (t // 4) if isinstance(t, int) else 4 * (t - u))
                    V.tensor_scalar(sidx[:, u:u + 1], xini[:, u, ID:ID + 1], -1.0, float(ID_BASE), ALU.mult, ALU.add)
                    V.scalar_tensor_tensor(yb[:, u, :], y_ps[u % 2], cy[:, 0:1],
                                           b2b[:, bass.ds(e, 1), :].rearrange("p a n -> p (a n)"),
                                           ALU.mult, ALU.add).then_inc(s["y_evac"], 1)

                copy_turned(0, 0)
                copy_turned(1, 1)

                def tile(t, u):
                    split_hidden(t, u % 2)
                    if not isinstance(t, int) or t + 2 < NT:
                        copy_turned(t + 2, u % 2)
                    if not isinstance(t, int) or t >= 1:
                        output(t - 1, (u - 1) % 4)

                for t in range(5):
                    tile(t, t % 4)
                with dve.Fori(5, 21, 4) as t:
                    for u in range(4):
                        tile(t + u, (1 + u) % 4)
                for t in range(21, NT):
                    tile(t, t % 4)
                output(NT - 1, (NT - 1) % 4)

            dve.wait_ge(consts_done, 1)
            dve.wait_ge(small_in, 16 * 4)
            res = lambda b: rows[:, 2 * b:2 * b + 2, RES:RES + D]
            for b in range(B + 1):
                if b < B:
                    if b % 2 == 0:
                        dve.wait_ge(x_in[b // 2], 16)
                    variance(res(b), b)
                if b >= 1:
                    normalise(res(b - 1), b - 1, "x")
                    keys(b - 1, b)
            route(0)

            dve.wait_ge(b1_turned, 1)
            V.tensor_reduce(wmax[:, 3:4], b1_ps, AX.X, ALU.max, apply_absolute_value=True).then_inc(maxes, 1)
            dve.wait_ge(w1_in, 16 * 4)
            V.tensor_reduce(wmax[:, 0:1], w1[:].rearrange("p e f -> p (e f)"), AX.X, ALU.max,
                            apply_absolute_value=True).then_inc(maxes, 1)
            dve.wait_ge(w2_in, 16 * 4)
            V.tensor_reduce(wmax[:, 1:2], w2[:].rearrange("p e c d -> p (e c d)"), AX.X, ALU.max,
                            apply_absolute_value=True).then_inc(maxes, 1)
            dve.wait_ge(wa_in, 16 * 10)
            V.tensor_reduce(wmax[:, 2:3], wa[:].rearrange("p e d -> p (e d)"), AX.X, ALU.max,
                            apply_absolute_value=True).then_inc(maxes, 1)
            dve.wait_ge(maxed, 1)
            step(V.tensor_tensor(gmax[:, 0:1], gmax[:, 0:1], gmax[:, 3:4], ALU.max))
            step(V.tensor_scalar(gmax[:], gmax[:], 1e-30, None, ALU.max))
            step(V.tensor_scalar(sexp[:].bitcast(I32), gmax[:].bitcast(I32), 0x7F800000, None, ALU.bitwise_and))
            step(V.tensor_scalar(sinv[:].bitcast(I32), sexp[:].bitcast(I32), -1.0, float(254 << 23), ALU.mult, ALU.add))
            V.tensor_scalar(sup[:], sinv[:], WTOP, None, ALU.mult).then_inc(scales, 1)
            step(V.tensor_scalar(s1h[:], sinv[:, 0:1], WTOP * HUNIT, None, ALU.mult))
            V.tensor_scalar(b1t[:].rearrange("p e c -> p (e c)"), b1_ps, s1h[:, 0:1], None, ALU.mult)
            V.tensor_scalar(cy[:], sexp[:, 0:1], sexp[:, 1:2], 0.5 / (HUNIT * WTOP * WTOP), ALU.mult, ALU.mult)
            V.tensor_scalar(ca[:], sexp[:, 2:3], 1.0 / (NSCALE * WTOP), None, ALU.mult)
            V.tensor_scalar(cg[:], sexp[:, 2:3], 0.5 / (NSCALE * WTOP), None, ALU.mult)
            V.tensor_scalar(b2b[:], b2b[:], 0.5, None, ALU.mult)
            V.tensor_scalar(wo[:], wo[:], 0.5, None, ALU.mult)
            V.tensor_scalar(bqg[:, 0:1], bqg[:, 0:1], 1.0, None, ALU.add)
            V.tensor_scalar(bqg[:, 1:2], bqg[:, 1:2], 0.5, None, ALU.mult)
            V.memset(minus_one[:], -1.0)
            step(V.tensor_scalar(bkv[:, 0, :], bkv[:, 0, :], 1.0, None, ALU.add))
            k = 0
            for full, high, low, g in ((w1, w1h, w1l, 0), (w2, w2h, w2l, 1)):
                for e in range(0, E, 2):
                    k += 1
                    dve.wait_ge(w_high, k)
                    fl = lambda a: a[:, e:e + 2].rearrange("p e f -> p (e f)" if g == 0 else "p e c d -> p (e c d)")
                    V.scalar_tensor_tensor(fl(low), fl(full), sup[:, g:g + 1], fl(high), ALU.mult,
                                           ALU.subtract).then_inc(w_low, 1)
            dve.wait_ge(w_high, 9)
            V.scalar_tensor_tensor(wal[:], wa[:], sup[:, 2:3], wah[:], ALU.mult, ALU.subtract).then_inc(w_low, 1)

            ffn(0)

            bkv2 = bkv[:].rearrange("p a n -> p (a n)")
            for i in range(TURNS):
                b, c, d = i - 1, i - 2, i - 3
                if 0 <= c < B:
                    k = c % 2
                    dve.wait_ge(kvh_done, c + 1)
                    if c >= 2:
                        dve.wait_ge(at_done, c - 1)
                    V.tensor_tensor(kvm[:, k], kvh_ps, headmask[:], ALU.mult).then_inc(kvm_ready, 1)
                if i < B:
                    if i % 2 == 0:
                        dve.wait_ge(x1_in[i // 2], 16)
                    variance(x1[:, 2 * i:2 * i + 2, :], i)
                if 0 <= d < B:
                    dve.wait_ge(o_done, d + 1)
                    dve.wait_ge(x1bo_ready, d + 1)
                    V.tensor_tensor(res(d), o_ps, x1bo[:, 2 * d:2 * d + 2, :], ALU.add).then_inc(x2_ready, 1)
                    dve.wait_ge(x2_ready, d + 1)
                    variance(res(d), d)
                if 0 <= b < B:
                    k = b % 2
                    dve.wait_ge(q_done, b + 1)
                    V.tensor_scalar(q1[:, k], q_ps, ca[:, 0:1], bqg[:, 0:1], ALU.mult, ALU.add).then_inc(q1_ready, 1)
                    dve.wait_ge(kv_done, b + 1)
                    if b >= 2:
                        dve.wait_ge(kvh_done, b - 1)
                    for j in range(PER_BATCH):
                        ins = V.scalar_tensor_tensor(kv1[:, k, j].rearrange("p a n -> p (a n)"),
                                                     kv_ps[:, j].rearrange("p a n -> p (a n)"), ca[:, 0:1], bkv2,
                                                     ALU.mult, ALU.add)
                    ins.then_inc(kv1_ready, 1)
                if 0 <= c < B:
                    k = c % 2
                    dve.wait_ge(at_done, c + 1)
                    dve.wait_ge(g_ready, c + 1)
                    if c >= 2:
                        dve.wait_ge(o_done, c - 1)
                    V.scalar_tensor_tensor(gat[:, k], gt[:, k], 1.0, at_ps, ALU.add, ALU.mult).then_inc(gated_ready, 1)
                if i < B:
                    normalise(x1[:, 2 * i:2 * i + 2, :], i, "attn")
                if 0 <= d < B:
                    normalise(res(d), d, "ffn")
                    keys(d, rsqrt_number("ffn", d))
                if 0 <= b < B:
                    k = b % 2
                    dve.wait_ge(qe_ready, b + 1)
                    if b >= 2:
                        dve.wait_ge(at_done, b - 1)
                    V.scalar_tensor_tensor(qt[:, k], qe[:, k], 1.0, q1[:, k], ALU.min, ALU.max).then_inc(q_ready, 1)
                    dve.wait_ge(ke_ready, b + 1)
                    V.scalar_tensor_tensor(kk[:, k], ke[:, k], 1.0, kv1[:, k, :, 0, :], ALU.min, ALU.max
                                           ).then_inc(k_ready, 1)
            route(1)
            ffn(1)
    return nc


_INS = ["L0_attn_x", "L0_attn_Wq", "L0_attn_bq", "L0_attn_Wk", "L0_attn_bk", "L0_attn_Wv", "L0_attn_bv",
        "L0_attn_Wg", "L0_attn_bg", "L0_attn_Wo", "L0_attn_bo", "L0_ffn_wr", "L0_ffn_br", "L0_ffn_W1",
        "L0_ffn_b1", "L0_ffn_W2", "L0_ffn_b2"]


def kernel(**inputs):
    import concourse.bacc as bacc
    from concourse.bass_utils import run_bass_kernel_spmd

    nc = bacc.Bacc("TRN2", target_bir_lowering=False, num_devices=1)
    arrays, args = {}, []
    for name in _INS:
        a = np.ascontiguousarray(inputs[name])
        if a.ndim == 0:
            a = a.reshape(1, 1)
        arrays[f"in_{name}"] = a
        args.append(nc.dram_tensor(f"in_{name}", a.shape, mybir.dt.from_np(a.dtype), kind="ExternalInput").ap())
    out = nc.dram_tensor("out", (B, S, D), FP32, kind="ExternalOutput").ap()
    sorted_rows = [nc.dram_tensor(f"sorted{f}", (NT * P, ROW), FP32, kind="Internal").ap() for f in range(2)]
    mid = nc.dram_tensor("mid", (TOKENS, D), FP32, kind="Internal").ap()
    build(nc, *args, out, sorted_rows, mid)
    r = run_bass_kernel_spmd(nc, [arrays], core_ids=[0])
    return r.results[0]["out"]
```

```python
from contextlib import ExitStack

import numpy as np
import concourse.bass as bass
from concourse import mybir

FP32, FP16, BF16 = mybir.dt.float32, mybir.dt.float16, mybir.dt.bfloat16
I32, U32 = mybir.dt.int32, mybir.dt.uint32
ALU = mybir.AluOpType
ACT = mybir.ActivationFunctionType
AX = mybir.AxisListType

P = 128
B, S, D = 8, 256, 128
E, F = 8, 512
TOKENS = B * S
TT = TOKENS // P
FC = F // P
NX = TT - 1
NT = E + NX
PER_BATCH = S // P
HEAD = 8
EPS = 1e-5
GROUPS = 4
GT = TT // GROUPS

ID, ROW = D, D + 4
ID_BASE = 4096
NSCALE = 4096.0
WTOP = 2.0 ** 14
HSCALE = 2.0 ** -19
HUNIT = HSCALE * NSCALE

HALF = F // 2
W1H, W1L, W2H, W2L = (k * F for k in range(4))
B1, B2, BLOCK = 4 * HALF, 4 * HALF + FC, 4 * HALF + FC + D
RING = 2 * E * F // BLOCK
AHEAD = 2


def build(nc, x_d, wq_d, bq_d, wk_d, bk_d, wv_d, bv_d, wg_d, bg_d, wo_d, bo_d,
          wr_d, br_d, w1_d, b1_d, w2_d, b2_d, out_d, sorted_d, y_d):
    ctx = ExitStack()
    with ctx:
        def sb(name, shape, dt=FP32):
            return ctx.enter_context(nc.sbuf_tensor(name, shape, dt))

        def ps(name, shape, dt=FP32):
            return ctx.enter_context(nc.psum_tensor(name, shape, dt))

        def sem(name):
            return ctx.enter_context(nc.semaphore(name))

        def fp16_view(t, n):
            return t[:].rearrange("p n w -> p (n w)").bitcast(FP16).rearrange("p (n w) -> p n w", n=n)

        xres = sb("xres", [P, TT, D])
        yin = sb("yin", [P, TT, D])
        norm = sb("norm", [P, TT, D])
        rows = sb("rows", [P, TT, ROW])
        rows16 = fp16_view(rows, TT)
        x1bo = sb("x1bo", [P, TT, D])
        stage = sb("stage", [P, 2 * E * F])
        w1 = stage[:, 0:E * F].rearrange("p (e f) -> p e f", e=E)
        w2 = stage[:, E * F:].rearrange("p (e f) -> p e f", e=E)
        ring = stage[:, 0:RING * BLOCK].rearrange("p (r w) -> p r w", r=RING)
        ring16 = stage[:, 0:RING * BLOCK].bitcast(FP16).rearrange("p (r w) -> p r w", r=RING)
        blocks = sb("blocks", [P, E, BLOCK])
        blocks16 = fp16_view(blocks, E)
        b1raw, b2raw = sb("b1raw", [E * FC, P]), sb("b2raw", [P, E, D])
        wa = sb("wa", [P, 4, D])
        wah, wal = sb("wah", [P, 4, D], FP16), sb("wal", [P, 4, D], FP16)
        wo, bqg, bkv, bob = sb("wo", [P, D]), sb("bqg", [P, 2]), sb("bkv", [P, 2, D]), sb("bob", [P, D])
        wrb, brb, wrsum = sb("wrb", [P, D]), sb("brb", [P, 1]), sb("wrsum", [P, 1])
        ident16, ident32 = sb("ident16", [P, P], FP16), sb("ident32", [P, P])
        before = sb("before", [P, P], BF16)
        ones16, ones32 = sb("ones16", [P, P], BF16), sb("ones32", [P, P])
        headmask = sb("headmask", [P, P])
        expert_no, first_slot = sb("expert_no", [P, E, TT]), sb("first_slot", [P, E, TT])
        extra_base = sb("extra_base", [P, E])
        extra_no = sb("extra_no", [P, NX, E])
        minus_half, minus_one = sb("minus_half", [P, TT]), sb("minus_one", [P, 1])
        zero_row = sb("zero_row", [P, ROW])
        stats = [sb(f"stats{k}", [P, TT, 6]) for k in range(3)]
        mv = [sb(f"mv{k}", [P, TT, 2]) for k in range(3)]
        var, varh = [sb(f"var{k}", [P, TT]) for k in range(3)], [sb(f"varh{k}", [P, TT]) for k in range(3)]
        rs0, rsq = [sb(f"rs0{k}", [P, TT]) for k in range(3)], [sb(f"rsq{k}", [P, TT]) for k in range(3)]
        rstd, shift = [sb(f"rstd{k}", [P, TT]) for k in range(3)], [sb(f"shift{k}", [P, TT]) for k in range(3)]
        dots = sb("dots", [P, TT])
        key, rk, rki, rgt = sb("key", [P, TT]), sb("rk", [P, TT]), sb("rki", [P, TT], I32), sb("rgt", [P, TT])
        rfl, rex = sb("rfl", [P, TT], I32), sb("rex", [P, TT], I32)
        onehot = sb("onehot", [P, E, TT], BF16)
        tot, scan = sb("tot", [P, E, TT]), sb("scan", [P, E, TT])
        pre, rank, beyond = sb("pre", [P, E, TT]), sb("rank", [P, E, TT]), sb("beyond", [P, E, TT])
        slot0, slot1, slot2 = sb("slot0", [P, E, TT]), sb("slot1", [P, E, TT]), sb("slot2", [P, E, TT])
        cnt, cnti, extra, extra_end = sb("cnt", [P, E]), sb("cnti", [P, E], I32), sb("extra", [P, E], I32), sb("extra_end", [P, E])
        adj0, adj = sb("adj0", [P, E]), sb("adj", [P, E])
        posf, pos = sb("posf", [P, TT]), sb("pos", [P, TT], I32)
        past, tef = sb("past", [P, NX, E]), sb("tef", [P, NX])
        te = [sb(f"te{f}", [P, NX], I32) for f in range(2)]
        wmax, wmaxt, wdiag = sb("wmax", [P, 4]), sb("wmaxt", [4, 1]), sb("wdiag", [4, 4])
        gmax, sexp, sinv, sup = sb("gmax", [P, 4]), sb("sexp", [P, 4]), sb("sinv", [P, 4]), sb("sup", [P, 4])
        cy, ca, cg, s1h = sb("cy", [P, 1]), sb("ca", [P, 1]), sb("cg", [P, 1]), sb("s1h", [P, 1])
        xin = sb("xin", [P, 6, ROW])
        xin16 = fp16_view(xin, 6)
        xini = xin[:].rearrange("p t w -> p (t w)").bitcast(I32).rearrange("p (t w) -> p t w", t=6)
        xt = sb("xt", [P, 3, 2, P], FP16)
        h32 = sb("h32", [P, 3, FC, P])
        hh, hl = sb("hh", [P, 3, FC, P], FP16), sb("hl", [P, 3, FC, P], FP16)
        ybuf, sidx = sb("ybuf", [P, 4, D]), sb("sidx", [P, 4], I32)
        nh2, nl2 = sb("nh2", [P, 2, PER_BATCH, D], FP16), sb("nl2", [P, 2, PER_BATCH, D], FP16)
        nt_sb = sb("nt_sb", [P, 2, 2, S], FP16)
        qe, qr, qm, qt = sb("qe", [P, 2, S]), sb("qr", [P, 2, S]), sb("qm", [P, 2, S]), sb("qt", [P, 2, S])
        gt, gat = sb("gt", [P, 2, S]), sb("gat", [P, 2, S])
        kv1 = sb("kv1", [P, 2, PER_BATCH, 2, D])
        ke, kk = sb("ke", [P, 2, PER_BATCH, D]), sb("kk", [P, 2, PER_BATCH, D])
        kvm = sb("kvm", [P, 2, P])

        bank = [ps(f"bank{i}", [P, 512]) for i in range(8)]
        xt_ps = [bank[i][:, 0:P].bitcast(FP16).rearrange("p (a n) -> p a n", a=2) for i in (0, 1)]
        h_ps = [bank[i][:].rearrange("p (c n) -> p c n", c=FC) for i in (2, 3, 7)]
        y_ps = [bank[i][:, 0:D] for i in (4, 5)]
        r_ps = bank[6][:, 0:2 * P].rearrange("p (a e t) -> p a e t", a=2, e=E)
        b1_ps, wmax_ps, gmax_ps = bank[7][:, 0:E * FC], bank[5][0:4, 0:P], bank[4][:, 0:4]
        nt_ps = bank[0][:, 0:S].bitcast(FP16).rearrange("p (a n) -> p a n", a=2)
        q_ps, g_ps = bank[1][:, 0:S], bank[7][:, 0:S]
        kv_ps = bank[2][:].rearrange("p (t a n) -> p t a n", t=PER_BATCH, a=2)
        kvh_ps = bank[3][:, 0:P]
        at_ps = bank[4][:, 0:S]
        o_ps = bank[5][:, 0:S].rearrange("p (t n) -> p t n", t=PER_BATCH)

        x_in = [sem(f"x_in{i}") for i in range(GROUPS)]
        y_in = [[sem(f"y_in{f}{i}") for i in range(GROUPS)] for f in range(2)]
        route_in, b1_in, b2_in, w_in, wa_in = sem("route_in"), sem("b1_in"), sem("b2_in"), [sem("w1_in"), sem("w2_in")], sem("wa_in")
        zero_set, filled = sem("zero_set"), [sem("filled0"), sem("filled1")]
        consts_done, dve_step, pool_step = sem("consts_done"), sem("dve_step"), sem("pool_step")
        b1_turned, wmax_ready, wmax_turned = sem("b1_turned"), sem("wmax_ready"), sem("wmax_turned")
        wdiag_ready, wmax_spread, scales = sem("wdiag_ready"), sem("wmax_spread"), sem("scales")
        bias_ready, w_high, w_low, wa_ready = sem("bias_ready"), sem("w_high"), sem("w_low"), sem("wa_ready")
        var_ready, pow_ready, rstd_ready = sem("var_ready"), sem("pow_ready"), sem("rstd_ready")
        row_high, row_low = sem("row_high"), sem("row_low")
        onehot_ready, ranked, routed = sem("onehot_ready"), sem("ranked"), sem("routed")
        L = [{n: sem(f"f{f}_{n}") for n in ("dispatched", "xt_done", "xt_copied", "h_done", "relu_done",
                                            "hh_done", "hl_done", "y_done", "y_evac")}
             | {"xin": [sem(f"f{f}_xin{u}") for u in range(6)],
                "weights": [sem(f"f{f}_weights{u}") for u in range(RING)],
                "stored": [sem(f"f{f}_stored{u}") for u in range(4)]} for f in range(2)]
        x1_ready, x1bo_ready, normed = sem("x1_ready"), sem("x1bo_ready"), sem("normed")
        n2_high, n2_low, nt_done, nt_copied = sem("n2_high"), sem("n2_low"), sem("nt_done"), sem("nt_copied")
        q_done, g_done, kv_done = sem("q_done"), sem("g_done"), sem("kv_done")
        qe_ready, qm_ready, q_ready, g_ready = sem("qe_ready"), sem("qm_ready"), sem("q_ready"), sem("g_ready")
        kv1_ready, ke_ready, k_ready = sem("kv1_ready"), sem("ke_ready"), sem("k_ready")
        kvh_done, kvm_ready, at_done, gated_ready = sem("kvh_done"), sem("kvm_ready"), sem("at_done"), sem("gated_ready")
        o_done, x2_ready, out_ready, out_stored = sem("o_done"), sem("x2_ready"), sem("out_ready"), sem("out_stored")

        block = ctx.enter_context(nc.Block())

        x_v = x_d.rearrange("b (h p) d -> p (b h) d", p=P)
        out_v = out_d.rearrange("b (h p) d -> p (b h) d", p=P)
        group = lambda i: slice(GT * i, GT * i + GT)
        ROOTS = [(0, 0, TT)] + [(1, GT * g, GT) for g in range(GROUPS)] + [(2, 0, TT // 2), (2, TT // 2, TT // 2)]
        TURNS = B + 3

        def tile_weights(t):
            if t < E:
                return blocks16[:, t], blocks[:, t]
            return ring16[:, (t - E) % RING], ring[:, (t - E) % RING]

        @block.sync
        def _(sp):
            for i in range(GROUPS):
                sp.dma_start(xres[:, group(i), :], x_v[:, group(i), :]).then_inc(x_in[i], 16)
                if i == 0:
                    sp.dma_start(wrb[:], wr_d.rearrange("(a n) -> a n", a=1).to_broadcast([P, D])).then_inc(route_in, 16)
                    sp.dma_start(brb[:], br_d.to_broadcast([P, 1])).then_inc(route_in, 16)
            sp.wait_ge(zero_set, 1)
            fill = lambda f: sp.dma_start(sorted_d[f].rearrange("(p k) w -> p k w", p=P),
                                          zero_row[:].rearrange("p (a w) -> p a w", a=1).to_broadcast([P, NT, ROW])
                                          ).then_inc(filled[f], 16)
            fill(0)
            sp.dma_start(b1raw[:], b1_d.rearrange("e (c p) -> (e c) p", p=P)).then_inc(b1_in, 16)
            for e in range(0, E, 2):
                sp.dma_start(w1[:, e:e + 2, :], w1_d[e:e + 2].rearrange("e p f -> p e f")).then_inc(w_in[0], 16)
            for e in range(0, E, 2):
                sp.dma_start(w2[:, e:e + 2, :].rearrange("p e (c d) -> p e c d", c=FC),
                             w2_d[e:e + 2].rearrange("e (c p) d -> p e c d", p=P)).then_inc(w_in[1], 16)
            for i, w in enumerate((wq_d, wg_d, wk_d, wv_d)):
                sp.dma_start(wa[:, i, :], w).then_inc(wa_in, 16)
            sp.dma_start(b2raw[:].rearrange("p e d -> p (e d)"),
                         b2_d.rearrange("(a e) d -> a (e d)", a=1).to_broadcast([P, E * D])).then_inc(b2_in, 16)
            sp.dma_start(wo[:], wo_d).then_inc(wa_in, 16)
            for i, b in enumerate((bq_d, bg_d)):
                sp.dma_start(bqg[:, i:i + 1], b.rearrange("(n a) -> n a", a=1)).then_inc(wa_in, 16)
            for i, b in enumerate((bk_d, bv_d)):
                sp.dma_start(bkv[:, i, :], b.rearrange("(a n) -> a n", a=1).to_broadcast([P, D])).then_inc(wa_in, 16)
            sp.dma_start(bob[:], bo_d.rearrange("(a n) -> a n", a=1).to_broadcast([P, D])).then_inc(wa_in, 16)
            fill(1)

            def ffn_loads(f):
                s = L[f]

                def weights(x):
                    if x >= RING:
                        sp.wait_ge(s["y_evac"], E + x - RING + 1)
                    e = sp.value_load(te[f][0:1, x:x + 1], min_val=0, max_val=E - 1)
                    sp.dma_start(ring[:, x % RING, :], blocks[:, bass.ds(e, 1), :].rearrange("p a w -> p (a w)")
                                 ).then_inc(s["weights"][x % RING], 16)

                sp.wait_ge(routed, f + 1)
                if f == 0:
                    sp.wait_ge(w_low, E)
                    sp.wait_ge(bias_ready, 1)
                if f == 1:
                    for x in range(RING):
                        weights(x)
                sp.wait_ge(s["dispatched"], 16 * TT)
                for t in range(NT):
                    if t >= 6:
                        sp.wait_ge(s["y_evac"], t - 5)
                    sp.dma_start(xin[:, t % 6, :], sorted_d[f][t * P:(t + 1) * P, :]).then_inc(s["xin"][t % 6], 16)
                    if f == 0 and t < RING:
                        weights(t)
                    late = t - 6 - (E - RING)
                    if RING <= late < NX:
                        weights(late)
                for u in range(4):
                    sp.wait_ge(s["stored"][u], 16 * len(range(u, NT, 4)))
                for i in range(GROUPS):
                    sp.dma_start(yin[:, group(i), :], y_d[f].rearrange("(t p) d -> p t d", p=P)[:, group(i), :]
                                 ).then_inc(y_in[f][i], 16)

            ffn_loads(0)
            ffn_loads(1)
            for i in range(GROUPS):
                sp.wait_ge(out_ready, i + 1)
                sp.dma_start(out_v[:, group(i), :], yin[:, group(i), :]).then_inc(out_stored, 16)
            sp.wait_ge(out_stored, 16 * GROUPS)

        @block.gpsimd
        def _(pool):
            n = [0]
            G = nc.gpsimd

            def step(ins):
                n[0] += 1
                ins.then_inc(pool_step, 1)
                pool.wait_ge(pool_step, n[0])

            G.memset(zero_row[:], 0.0).then_inc(zero_set, 1)
            G.memset(minus_half[:], -0.5)
            G.memset(ident16[:], 0.0)
            G.memset(ident32[:], 0.0)
            G.memset(ones16[:], 1.0)
            G.memset(ones32[:], 1.0)
            G.memset(before[:], 0.0)
            G.memset(rows[:, :, ID + 1:ROW], 0.0)
            step(G.memset(headmask[:], 1.0))
            G.iota(rows[:].bitcast(I32)[:, :, ID:ID + 1], pattern=[[-P, TT]], base=ID_BASE, channel_multiplier=-1)
            small = dict(channel_multiplier=0, allow_small_or_imprecise_dtypes=True)
            G.iota(expert_no[:], pattern=[[1, E], [0, TT]], base=0, **small)
            G.iota(first_slot[:], pattern=[[P, E], [0, TT]], base=0, **small)
            G.iota(extra_base[:], pattern=[[-P, E]], base=P * E - P, **small)
            G.iota(extra_no[:], pattern=[[1, NX], [0, E]], base=0, **small)
            for m in (ident16, ident32):
                G.affine_select(out=m[:], in_=m[:], compare_op=ALU.not_equal, fill=1.0, base=0,
                                pattern=[[-1, P]], channel_multiplier=1)
            G.affine_select(out=before[:], in_=before[:], compare_op=ALU.is_ge, fill=1.0, base=0,
                            pattern=[[-1, P]], channel_multiplier=1)
            hm = headmask[:].rearrange("p (g n) -> p g n", n=HEAD)
            step(G.affine_select(out=hm, in_=hm, compare_op=ALU.is_ge, fill=0.0, base=0,
                                 pattern=[[-HEAD, P // HEAD], [0, HEAD]], channel_multiplier=1))
            G.affine_select(out=hm, in_=hm, compare_op=ALU.is_ge, fill=0.0, base=HEAD - 1,
                            pattern=[[HEAD, P // HEAD], [0, HEAD]], channel_multiplier=-1).then_inc(consts_done, 1)

            def root(k):
                ln, t, m = ROOTS[k]
                pool.wait_ge(var_ready, k + 1)
                G.tensor_tensor(rs0[ln][:, t:t + m], var[ln][:, t:t + m], minus_half[:, t:t + m], ALU.pow
                                ).then_inc(pow_ready, 1)

            def row_lows(f, b):
                pool.wait_ge(row_high, B * f + b + 1)
                v = slice(PER_BATCH * b, PER_BATCH * (b + 1))
                G.tensor_tensor(rows16[:, v, D:2 * D], norm[:, v, :], rows16[:, v, 0:D],
                                ALU.subtract).then_inc(row_low, 1)

            def dispatch(f):
                pool.wait_ge(filled[f], 16)
                pool.wait_ge(routed, f + 1)
                pool.wait_ge(row_low, (f + 1) * B)
                for j in range(TT):
                    G.indirect_dma_start(
                        sorted_d[f], bass.IndirectOffsetOnAxis(ap=pos[:, j:j + 1].bitcast(U32), axis=0),
                        rows[:, j, :], None).then_inc(L[f]["dispatched"], 16)

            def collect(f):
                s = L[f]
                for t in range(NT):
                    u = t % 4
                    pool.wait_ge(s["y_evac"], t + 1)
                    G.indirect_dma_start(
                        y_d[f], bass.IndirectOffsetOnAxis(ap=sidx[:, u:u + 1].bitcast(U32), axis=0),
                        ybuf[:, u, :], None, bounds_check=TOKENS - 1, oob_is_err=False).then_inc(s["stored"][u], 16)

            def attention_lows(b):
                pool.wait_ge(n2_high, b + 1)
                if b >= 2:
                    pool.wait_ge(nt_done, b - 1)
                G.tensor_tensor(nl2[:, b % 2], norm[:, PER_BATCH * b:PER_BATCH * (b + 1), :], nh2[:, b % 2],
                                ALU.subtract).then_inc(n2_low, 1)

            root(0)
            for b in range(B):
                row_lows(0, b)
            dispatch(0)
            collect(0)
            root(1)
            root(2)
            attention_lows(0)
            for i in range(TURNS):
                b = i - 1
                if i + 3 <= GROUPS:
                    root(i + 3)
                if i + 1 < B:
                    attention_lows(i + 1)
                if 0 <= b < B:
                    k = b % 2
                    pool.wait_ge(qe_ready, b + 1)
                    G.tensor_scalar(qm[:, k], qe[:, k], 1.0, None, ALU.min).then_inc(qm_ready, 1)
                    pool.wait_ge(qm_ready, b + 1)
                    if b >= 2:
                        pool.wait_ge(at_done, b - 1)
                    G.tensor_tensor(qt[:, k], qm[:, k], qr[:, k], ALU.add).then_inc(q_ready, 1)
                if i < B:
                    v = slice(PER_BATCH * i, PER_BATCH * (i + 1))
                    pool.wait_ge(x1_ready, i // PER_BATCH + 1)
                    G.tensor_tensor(x1bo[:, v, :], xres[:, v, :],
                                    bob[:].rearrange("p (a n) -> p a n", a=1).to_broadcast([P, PER_BATCH, D]),
                                    ALU.add).then_inc(x1bo_ready, 1)
                if i == B // 2 + 3:
                    root(5)
                    for b in range(B // 2):
                        row_lows(1, b)
            root(6)
            for b in range(B // 2, B):
                row_lows(1, b)
            dispatch(1)
            collect(1)

        @block.scalar
        def _(act):
            A = nc.scalar

            def normalise(ln, b, done):
                for j in range(PER_BATCH * b, PER_BATCH * (b + 1)):
                    ins = A.activation(norm[:, j, :], xres[:, j, :], ACT.Identity, bias=shift[ln][:, j:j + 1],
                                       scale=rstd[ln][:, j:j + 1])
                ins.then_inc(normed, 1)
                act.wait_ge(normed, done)

            def row_highs(f, b):
                normalise(2 * f, b, (2 * B if f else 0) + b + 1)
                v = slice(PER_BATCH * b, PER_BATCH * (b + 1))
                A.activation(rows16[:, v, 0:D], norm[:, v, :], ACT.Copy).then_inc(row_high, 1)

            act.wait_ge(rstd_ready, 1)
            for b in range(B):
                row_highs(0, b)
            act.wait_ge(scales, 1)
            for e in range(0, E, 2):
                A.activation(blocks16[:, e:e + 2, W1H:W1H + F], w1[:, e:e + 2, :], ACT.Copy, scale=sup[:, 0:1])
                A.activation(blocks16[:, e:e + 2, W2H:W2H + F], w2[:, e:e + 2, :], ACT.Copy, scale=sup[:, 1:2]
                             ).then_inc(w_high, 2)
            A.activation(wah[:], wa[:], ACT.Copy, scale=sup[:, 2:3]).then_inc(w_high, 1)

            def ffn(f):
                s = L[f]

                def copy_turned(t):
                    act.wait_ge(s["xt_done"], t + 1)
                    if t >= 3:
                        act.wait_ge(s["h_done"], t - 2)
                    A.activation(xt[:, t % 3], xt_ps[t % 2], ACT.Copy).then_inc(s["xt_copied"], 1)

                def hidden(t):
                    act.wait_ge(s["h_done"], t + 1)
                    if t >= 3:
                        act.wait_ge(s["hl_done"], t - 2)
                    _, w = tile_weights(t)
                    for c in range(FC):
                        ins = A.activation(h32[:, t % 3, c, :], h_ps[t % 3][:, c, :], ACT.Relu,
                                           bias=w[:, B1 + c:B1 + c + 1], scale=HSCALE)
                    ins.then_inc(s["relu_done"], 1)

                if f == 0:
                    act.wait_ge(bias_ready, 1)
                for t in range(AHEAD + 1):
                    copy_turned(t)
                for t in range(AHEAD):
                    hidden(t)
                for t in range(NT):
                    if t + AHEAD < NT:
                        hidden(t + AHEAD)
                    if t + AHEAD + 1 < NT:
                        copy_turned(t + AHEAD + 1)

            def attention_highs(b):
                if b % PER_BATCH == 0:
                    act.wait_ge(rstd_ready, 2 + b // PER_BATCH)
                normalise(1, b, B + b + 1)
                if b >= 2:
                    act.wait_ge(nt_done, b - 1)
                A.activation(nh2[:, b % 2], norm[:, PER_BATCH * b:PER_BATCH * (b + 1), :], ACT.Copy
                             ).then_inc(n2_high, 1)

            ffn(0)
            attention_highs(0)
            for i in range(TURNS):
                b = i - 1
                if i < B:
                    act.wait_ge(nt_done, i + 1)
                    if i >= 2:
                        act.wait_ge(kv_done, i - 1)
                    A.activation(nt_sb[:, i % 2], nt_ps, ACT.Copy).then_inc(nt_copied, 1)
                if 0 <= b < B:
                    k = b % 2
                    act.wait_ge(q_done, b + 1)
                    if b >= 2:
                        act.wait_ge(q_ready, b - 1)
                    A.activation(qe[:, k], q_ps, ACT.Exp, bias=bqg[:, 0:1], scale=ca[:, 0:1])
                    A.activation(qr[:, k], q_ps, ACT.Relu, bias=bqg[:, 0:1], scale=ca[:, 0:1]).then_inc(qe_ready, 1)
                    act.wait_ge(kv1_ready, b + 1)
                    if b >= 2:
                        act.wait_ge(k_ready, b - 1)
                    A.activation(ke[:, k], kv1[:, k, :, 0, :], ACT.Exp, bias=minus_one[:, 0:1]).then_inc(ke_ready, 1)
                    act.wait_ge(g_done, b + 1)
                    if b >= 2:
                        act.wait_ge(gated_ready, b - 1)
                    A.activation(gt[:, k], g_ps, ACT.Tanh, bias=bqg[:, 1:2], scale=cg[:, 0:1]).then_inc(g_ready, 1)
                if i + 1 < B:
                    attention_highs(i + 1)
                if i == B // 2 + 3:
                    act.wait_ge(rstd_ready, 6)
                    for b in range(B // 2):
                        row_highs(1, b)
            act.wait_ge(rstd_ready, 7)
            for b in range(B // 2, B):
                row_highs(1, b)
            ffn(1)

        @block.tensor
        def _(pe):
            MM, T = nc.tensor.matmul, nc.tensor.transpose

            def split_matmul(out, whi, wlo, xhi, xlo):
                MM(out, whi, xhi, start=True, stop=False)
                MM(out, whi, xlo, start=False, stop=False)
                return MM(out, wlo, xhi, start=False, stop=True)

            def rank_tokens(f):
                pe.wait_ge(onehot_ready, f + 1)
                oh = onehot[:].rearrange("p e t -> p (e t)")
                MM(r_ps[:, 1].rearrange("p e t -> p (e t)"), ones16[:], oh, start=True, stop=True)
                MM(r_ps[:, 0].rearrange("p e t -> p (e t)"), before[:], oh, start=True, stop=True).then_inc(ranked, 1)

            def ffn(f):
                s = L[f]

                def turn(t):
                    pe.wait_ge(s["xin"][t % 6], 16 * (t // 6 + 1))
                    if t >= 2:
                        pe.wait_ge(s["xt_copied"], t - 1)
                    for a in range(2):
                        ins = T(xt_ps[t % 2][:, a, :], xin16[:, t % 6, a * D:(a + 1) * D], ident16[:])
                    ins.then_inc(s["xt_done"], 1)

                def first(t):
                    w, _ = tile_weights(t)
                    pe.wait_ge(s["xt_copied"], t + 1)
                    if t >= 3:
                        pe.wait_ge(s["relu_done"], t - 2)
                    if t < E:
                        if f == 0:
                            pe.wait_ge(w_low, t + 1)
                    else:
                        x = t - E
                        pe.wait_ge(s["weights"][x % RING], 16 * (x // RING + 1))
                    for c in range(FC):
                        hi, lo = (w[:, o + c * P:o + (c + 1) * P] for o in (W1H, W1L))
                        ins = split_matmul(h_ps[t % 3][:, c, :], hi, lo, xt[:, t % 3, 0, :], xt[:, t % 3, 1, :])
                    ins.then_inc(s["h_done"], 1)

                def second(t):
                    w, _ = tile_weights(t)
                    pe.wait_ge(s["hl_done"], t + 1)
                    if t >= 2:
                        pe.wait_ge(s["y_evac"], t - 1)
                    out = y_ps[t % 2]
                    for c in range(FC):
                        hi, lo = (w[:, o + c * D:o + (c + 1) * D] for o in (W2H, W2L))
                        MM(out, hh[:, t % 3, c, :], hi, start=(c == 0), stop=False)
                        MM(out, hh[:, t % 3, c, :], lo, start=False, stop=False)
                        ins = MM(out, hl[:, t % 3, c, :], hi, start=False, stop=(c == FC - 1))
                    ins.then_inc(s["y_done"], 1)

                for t in range(AHEAD + 1):
                    turn(t)
                for t in range(AHEAD):
                    first(t)
                for t in range(NT):
                    if t + AHEAD < NT:
                        first(t + AHEAD)
                    if t + AHEAD + 1 < NT:
                        turn(t + AHEAD + 1)
                    second(t)

            pe.wait_ge(consts_done, 1)
            rank_tokens(0)
            pe.wait_ge(b1_in, 16)
            T(b1_ps, b1raw[:], ident32[0:E * FC, 0:E * FC]).then_inc(b1_turned, 1)
            pe.wait_ge(wmax_ready, 1)
            T(wmax_ps, wmax[:], ident32[:]).then_inc(wmax_turned, 1)
            pe.wait_ge(wdiag_ready, 1)
            MM(gmax_ps, ones32[0:4, :], wdiag[:], start=True, stop=True).then_inc(wmax_spread, 1)
            ffn(0)
            for i in range(TURNS):
                c = i - 2
                if 0 <= c < B:
                    k = c % 2
                    pe.wait_ge(k_ready, c + 1)
                    if c >= 1:
                        pe.wait_ge(kvm_ready, c)
                    for j in range(PER_BATCH):
                        ins = MM(kvh_ps, kk[:, k, j, :], kv1[:, k, j, 1, :], start=(j == 0), stop=(j == PER_BATCH - 1))
                    ins.then_inc(kvh_done, 1)
                if i < B:
                    k = i % 2
                    pe.wait_ge(n2_high, i + 1)
                    pe.wait_ge(n2_low, i + 1)
                    if i >= 1:
                        pe.wait_ge(nt_copied, i)
                    for j in range(PER_BATCH):
                        for a, src in enumerate((nh2, nl2)):
                            ins = T(nt_ps[:, a, j * P:(j + 1) * P], src[:, k, j, :], ident16[:])
                    ins.then_inc(nt_done, 1)
                if 0 <= c < B:
                    k = c % 2
                    pe.wait_ge(kvm_ready, c + 1)
                    pe.wait_ge(q_ready, c + 1)
                    if c >= 1:
                        pe.wait_ge(gated_ready, c)
                    MM(at_ps, kvm[:, k], qt[:, k], start=True, stop=True).then_inc(at_done, 1)
                if i < B:
                    k = i % 2
                    if i == 0:
                        pe.wait_ge(wa_ready, 1)
                    pe.wait_ge(nt_copied, i + 1)
                    if i >= 1:
                        pe.wait_ge(qe_ready, i)
                        pe.wait_ge(g_ready, i)
                    split_matmul(q_ps, wah[:, 0, :], wal[:, 0, :], nt_sb[:, k, 0, :], nt_sb[:, k, 1, :]).then_inc(q_done, 1)
                    if i >= 1:
                        pe.wait_ge(kv1_ready, i)
                    kvh, kvl = (w[:, 2:4, :].rearrange("p a n -> p (a n)") for w in (wah, wal))
                    for j in range(PER_BATCH):
                        out = kv_ps[:, j].rearrange("p a n -> p (a n)")
                        th, tl = (nt_sb[:, k, a, j * P:(j + 1) * P] for a in range(2))
                        MM(out, th, kvh, start=True, stop=False)
                        MM(out, th, kvl, start=False, stop=False)
                        ins = MM(out, tl, kvh, start=False, stop=True)
                    ins.then_inc(kv_done, 1)
                    split_matmul(g_ps, wah[:, 1, :], wal[:, 1, :], nt_sb[:, k, 0, :], nt_sb[:, k, 1, :]).then_inc(g_done, 1)
                if 0 <= c < B:
                    k = c % 2
                    pe.wait_ge(gated_ready, c + 1)
                    if c >= 1:
                        pe.wait_ge(x2_ready, c)
                    for j in range(PER_BATCH):
                        ins = MM(o_ps[:, j, :], gat[:, k, j * P:(j + 1) * P], wo[:], start=True, stop=True)
                    ins.then_inc(o_done, 1)
            rank_tokens(1)
            ffn(1)

        @block.vector
        def _(dve):
            n = [0]
            V = nc.vector

            def step(ins):
                n[0] += 1
                ins.then_inc(dve_step, 1)
                dve.wait_ge(dve_step, n[0])

            def tile_stats(ln, t, m):
                for j in range(t, t + m):
                    ins = V.bn_stats(stats[ln][:, j, :], xres[:, j, :])
                return ins

            def tile_dots(t, m):
                for j in range(t, t + m):
                    ins = V.tensor_tensor_reduce(out=norm[:, j, :], in0=xres[:, j, :], in1=wrb[:], scale=1.0,
                                                 scalar=0.0, op0=ALU.mult, op1=ALU.add, accum_out=dots[:, j:j + 1])
                return ins

            def variance(ln, t, m):
                for j in range(t, t + m):
                    ins = V.bn_aggr(mv[ln][:, j, :], stats[ln][:, j, :])
                step(ins)
                V.tensor_scalar(var[ln][:, t:t + m], mv[ln][:, t:t + m, 1], EPS, None, ALU.add).then_inc(var_ready, 1)
                V.tensor_scalar(varh[ln][:, t:t + m], mv[ln][:, t:t + m, 1], EPS, -0.5 * NSCALE, ALU.add, ALU.mult)

            def inverse_root(k):
                ln, t, m = ROOTS[k]
                v = slice(t, t + m)
                dve.wait_ge(pow_ready, k + 1)
                step(V.tensor_tensor(rsq[ln][:, v], rs0[ln][:, v], rs0[ln][:, v], ALU.mult))
                step(V.tensor_tensor(varh[ln][:, v], rsq[ln][:, v], varh[ln][:, v], ALU.mult))
                step(V.scalar_tensor_tensor(rstd[ln][:, v], varh[ln][:, v], 1.5 * NSCALE, rs0[ln][:, v], ALU.add, ALU.mult))
                V.scalar_tensor_tensor(shift[ln][:, v], mv[ln][:, v, 0], -1.0, rstd[ln][:, v], ALU.mult, ALU.mult
                                       ).then_inc(rstd_ready, 1)

            def route(f):
                ln = 2 * f
                step(V.scalar_tensor_tensor(key[:], mv[ln][:, :, 0], wrsum[:, 0:1], dots[:], ALU.mult, ALU.subtract))
                step(V.tensor_tensor(rgt[:], key[:], rstd[ln][:], ALU.mult))
                V.tensor_scalar(rki[:], rgt[:], -1.0 / NSCALE, brb[:, 0:1], ALU.mult, ALU.add)
                step(V.tensor_scalar(rk[:], rgt[:], -1.0 / NSCALE, brb[:, 0:1], ALU.mult, ALU.add))
                step(V.tensor_tensor(rgt[:], rki[:], rk[:], ALU.is_gt))
                step(V.tensor_tensor(rfl[:], rki[:], rgt[:], ALU.subtract))
                step(V.tensor_scalar(rex[:], rfl[:], E - 1, None, ALU.bitwise_and))
                V.tensor_tensor(onehot[:], rex[:].rearrange("p (a t) -> p a t", a=1).to_broadcast([P, E, TT]),
                                expert_no[:], ALU.is_equal).then_inc(onehot_ready, 1)
                dve.wait_ge(ranked, f + 1)
                flat = lambda a: a[:].rearrange("p e t -> p (e t)")
                by_expert = lambda a: a[:].rearrange("p (e o) -> p e o", o=1).to_broadcast([P, E, TT])
                V.tensor_copy(tot[:], r_ps[:, 1])
                step(V.tensor_reduce(cnt[:], r_ps[:, 1], AX.X, ALU.add))
                V.tensor_scalar(cnti[:], cnt[:], float(P), -1.0, ALU.max, ALU.add)
                step(V.tensor_tensor_scan(flat(scan), ones32[:], flat(tot), 0.0, ALU.mult, ALU.add))
                V.tensor_scalar(extra[:], cnti[:], 7, None, ALU.logical_shift_right)
                step(V.tensor_tensor(pre[:], scan[:], tot[:], ALU.subtract))
                step(V.tensor_tensor_scan(extra_end[:], ones32[:, 0:E], extra[:], 0.0, ALU.mult, ALU.add))
                V.tensor_tensor(rank[:], pre[:], pre[:, :, 0:1].to_broadcast([P, E, TT]), ALU.subtract)
                step(V.tensor_tensor(adj0[:], extra_end[:], extra[:], ALU.subtract))
                V.scalar_tensor_tensor(adj[:], adj0[:], float(P), extra_base[:], ALU.mult, ALU.add)
                step(V.tensor_tensor(rank[:], rank[:], r_ps[:, 0], ALU.add))
                V.scalar_tensor_tensor(beyond[:], rank[:], float(P), by_expert(adj), ALU.is_ge, ALU.mult)
                step(V.tensor_tensor(slot0[:], rank[:], first_slot[:], ALU.add))
                step(V.tensor_tensor(slot1[:], slot0[:], beyond[:], ALU.add))
                step(V.tensor_tensor(slot2[:], slot1[:], onehot[:], ALU.mult))
                V.tensor_tensor(past[:], extra_no[:], extra_end[:].rearrange("p (a e) -> p a e", a=1).to_broadcast([P, NX, E]),
                                ALU.is_ge)
                step(V.tensor_reduce(posf[:], slot2[:].rearrange("p e t -> p t e"), AX.X, ALU.add))
                V.tensor_copy(pos[:], posf[:])
                step(V.tensor_reduce(tef[:], past[:], AX.X, ALU.add))
                V.tensor_scalar(te[f][:], tef[:], float(E - 1), None, ALU.min).then_inc(routed, 1)

            def ffn(f):
                s = L[f]

                def split_hidden(t):
                    k = t % 3
                    dve.wait_ge(s["relu_done"], t + 1)
                    if t >= 3:
                        dve.wait_ge(s["y_done"], t - 2)
                    V.tensor_copy(hh[:, k], h32[:, k]).then_inc(s["hh_done"], 1)
                    dve.wait_ge(s["hh_done"], t + 1)
                    V.tensor_tensor(hl[:, k], h32[:, k], hh[:, k], ALU.subtract).then_inc(s["hl_done"], 1)

                def output(t):
                    u = t % 4
                    dve.wait_ge(s["y_done"], t + 1)
                    if t >= 4:
                        dve.wait_ge(s["stored"][u], 16 * (t // 4))
                    V.tensor_scalar(sidx[:, u:u + 1], xini[:, t % 6, ID:ID + 1], -1.0, float(ID_BASE), ALU.mult, ALU.add)
                    _, w = tile_weights(t)
                    V.scalar_tensor_tensor(ybuf[:, u, :], y_ps[t % 2], cy[:, 0:1], w[:, B2:B2 + D],
                                           ALU.mult, ALU.add).then_inc(s["y_evac"], 1)

                for t in range(AHEAD):
                    split_hidden(t)
                for t in range(NT):
                    if t >= 1:
                        output(t - 1)
                    if t + AHEAD < NT:
                        split_hidden(t + AHEAD)
                output(NT - 1)

            dve.wait_ge(x_in[0], 16)
            tile_stats(0, 0, GT)
            dve.wait_ge(route_in, 32)
            step(V.tensor_reduce(wrsum[:], wrb[:], AX.X, ALU.add))
            for i in range(1, GROUPS):
                dve.wait_ge(x_in[i], 16)
                ins = tile_stats(0, GT * i, GT)
            step(ins)
            variance(0, 0, TT)
            step(tile_dots(0, TT))
            inverse_root(0)
            dve.wait_ge(rstd_ready, 1)
            dve.wait_ge(consts_done, 1)
            route(0)

            absmax = lambda out, a: V.tensor_reduce(out, a, AX.X, ALU.max, apply_absolute_value=True)
            dve.wait_ge(b1_turned, 1)
            step(absmax(wmax[:, 3:4], b1_ps))
            for i, w in enumerate((w1, w2)):
                dve.wait_ge(w_in[i], 16 * 4)
                absmax(wmax[:, i:i + 1], w.rearrange("p e f -> p (e f)"))
            dve.wait_ge(wa_in, 16 * 10)
            step(absmax(wmax[:, 2:3], wa[:].rearrange("p e d -> p (e d)")))
            V.tensor_tensor(wmax[:, 0:1], wmax[:, 0:1], wmax[:, 3:4], ALU.max).then_inc(wmax_ready, 1)
            dve.wait_ge(wmax_turned, 1)
            step(V.tensor_reduce(wmaxt[:], wmax_ps, AX.X, ALU.max))
            V.tensor_scalar(wdiag[:], ident32[0:4, 0:4], wmaxt[:, 0:1], None, ALU.mult).then_inc(wdiag_ready, 1)
            dve.wait_ge(wmax_spread, 1)
            step(V.tensor_scalar(gmax[:], gmax_ps, 1e-30, None, ALU.max))
            step(V.tensor_scalar(sexp[:].bitcast(I32), gmax[:].bitcast(I32), 0x7F800000, None, ALU.bitwise_and))
            step(V.tensor_scalar(sinv[:].bitcast(I32), sexp[:].bitcast(I32), -1.0, float(254 << 23), ALU.mult, ALU.add))
            V.tensor_scalar(sup[:], sinv[:], WTOP, None, ALU.mult).then_inc(scales, 1)
            step(V.tensor_scalar(s1h[:], sinv[:, 0:1], WTOP * HUNIT, None, ALU.mult))
            V.tensor_scalar(blocks[:, :, B1:B1 + FC], b1_ps.rearrange("p (e c) -> p e c", e=E), s1h[:, 0:1], None, ALU.mult)
            V.tensor_scalar(cy[:], sexp[:, 0:1], sexp[:, 1:2], None, ALU.mult)
            dve.wait_ge(b2_in, 16)
            step(V.tensor_scalar(blocks[:, :, B2:B2 + D], b2raw[:], 0.5, None, ALU.mult))
            V.tensor_scalar(cy[:], cy[:], 0.5 / (HUNIT * WTOP * WTOP), None, ALU.mult).then_inc(bias_ready, 1)
            for e in range(0, E, 2):
                dve.wait_ge(w_high, e + 2)
                for w, h, l, g in ((w1, W1H, W1L, 0), (w2, W2H, W2L, 1)):
                    ins = V.scalar_tensor_tensor(blocks16[:, e:e + 2, l:l + F], w[:, e:e + 2, :], sup[:, g:g + 1],
                                                 blocks16[:, e:e + 2, h:h + F], ALU.mult, ALU.subtract)
                ins.then_inc(w_low, 2)
            dve.wait_ge(w_high, E + 1)
            V.scalar_tensor_tensor(wal[:], wa[:], sup[:, 2:3], wah[:], ALU.mult, ALU.subtract)
            V.tensor_scalar(ca[:], sexp[:, 2:3], 1.0 / (NSCALE * WTOP), None, ALU.mult)
            V.tensor_scalar(cg[:], sexp[:, 2:3], 0.5 / (NSCALE * WTOP), None, ALU.mult)
            V.tensor_scalar(wo[:], wo[:], 0.5, None, ALU.mult)
            V.tensor_scalar(bqg[:, 1:2], bqg[:, 1:2], 0.5, None, ALU.mult)
            V.memset(minus_one[:], -1.0)
            V.tensor_scalar(bkv[:, 0, :], bkv[:, 0, :], 1.0, None, ALU.add).then_inc(wa_ready, 1)

            ffn(0)

            def attention_input(g):
                dve.wait_ge(y_in[0][g], 16)
                V.tensor_tensor(xres[:, group(g), :], xres[:, group(g), :], yin[:, group(g), :], ALU.add
                                ).then_inc(x1_ready, 1)
                dve.wait_ge(x1_ready, g + 1)
                step(tile_stats(1, GT * g, GT))
                variance(1, GT * g, GT)

            bkv2 = bkv[:].rearrange("p a n -> p (a n)")
            dve.wait_ge(wa_ready, 1)
            attention_input(0)
            attention_input(1)
            inverse_root(1)
            for i in range(TURNS):
                b, c, d = i - 1, i - 2, i - 3
                if i < GROUPS - 1:
                    if i + 2 < GROUPS:
                        attention_input(i + 2)
                    inverse_root(i + 2)
                if 0 <= c < B:
                    k = c % 2
                    dve.wait_ge(kvh_done, c + 1)
                    V.tensor_tensor(kvm[:, k], kvh_ps, headmask[:], ALU.mult).then_inc(kvm_ready, 1)
                if 0 <= b < B:
                    k = b % 2
                    dve.wait_ge(kv_done, b + 1)
                    for j in range(PER_BATCH):
                        ins = V.scalar_tensor_tensor(kv1[:, k, j].rearrange("p a n -> p (a n)"),
                                                     kv_ps[:, j].rearrange("p a n -> p (a n)"), ca[:, 0:1], bkv2,
                                                     ALU.mult, ALU.add)
                    ins.then_inc(kv1_ready, 1)
                if 0 <= d < B:
                    v = slice(PER_BATCH * d, PER_BATCH * (d + 1))
                    dve.wait_ge(o_done, d + 1)
                    dve.wait_ge(x1bo_ready, d + 1)
                    V.tensor_tensor(xres[:, v, :], o_ps, x1bo[:, v, :], ALU.add).then_inc(x2_ready, 1)
                if 0 <= c < B:
                    k = c % 2
                    dve.wait_ge(at_done, c + 1)
                    dve.wait_ge(g_ready, c + 1)
                    V.scalar_tensor_tensor(gat[:, k], gt[:, k], 1.0, at_ps, ALU.add, ALU.mult).then_inc(gated_ready, 1)
                if 0 <= b < B:
                    k = b % 2
                    dve.wait_ge(ke_ready, b + 1)
                    V.scalar_tensor_tensor(kk[:, k], ke[:, k], 1.0, kv1[:, k, :, 0, :], ALU.min, ALU.max
                                           ).then_inc(k_ready, 1)
                if 0 <= d < B:
                    dve.wait_ge(x2_ready, d + 1)
                    tile_stats(2, PER_BATCH * d, PER_BATCH)
                    ins = tile_dots(PER_BATCH * d, PER_BATCH)
                    if d == B // 2 - 1:
                        step(ins)
                        variance(2, 0, TT // 2)
                if i == B // 2 + 3:
                    inverse_root(5)
            step(ins)
            variance(2, TT // 2, TT // 2)
            inverse_root(6)
            dve.wait_ge(rstd_ready, 7)
            route(1)
            ffn(1)
            for g in range(GROUPS):
                dve.wait_ge(y_in[1][g], 16)
                V.tensor_tensor(yin[:, group(g), :], xres[:, group(g), :], yin[:, group(g), :], ALU.add
                                ).then_inc(out_ready, 1)
    return nc


_INS = ["L0_attn_x", "L0_attn_Wq", "L0_attn_bq", "L0_attn_Wk", "L0_attn_bk", "L0_attn_Wv", "L0_attn_bv",
        "L0_attn_Wg", "L0_attn_bg", "L0_attn_Wo", "L0_attn_bo", "L0_ffn_wr", "L0_ffn_br", "L0_ffn_W1",
        "L0_ffn_b1", "L0_ffn_W2", "L0_ffn_b2"]


def kernel(**inputs):
    import concourse.bacc as bacc
    from concourse.bass_utils import run_bass_kernel_spmd

    nc = bacc.Bacc("TRN2", target_bir_lowering=False, num_devices=1)
    arrays, args = {}, []
    for name in _INS:
        a = np.ascontiguousarray(inputs[name])
        if a.ndim == 0:
            a = a.reshape(1, 1)
        arrays[f"in_{name}"] = a
        args.append(nc.dram_tensor(f"in_{name}", a.shape, mybir.dt.from_np(a.dtype), kind="ExternalInput").ap())
    out = nc.dram_tensor("out", (B, S, D), FP32, kind="ExternalOutput").ap()
    sorted_rows = [nc.dram_tensor(f"sorted{f}", (NT * P, ROW), FP32, kind="Internal").ap() for f in range(2)]
    ys = [nc.dram_tensor(f"y{f}", (TOKENS, D), FP32, kind="Internal").ap() for f in range(2)]
    build(nc, *args, out, sorted_rows, ys)
    r = run_bass_kernel_spmd(nc, [arrays], core_ids=[0])
    return r.results[0]["out"]
```

```python
from contextlib import ExitStack
from itertools import chain, islice

import numpy as np
import concourse.bass as bass
from concourse import mybir

FP32, FP16, BF16 = mybir.dt.float32, mybir.dt.float16, mybir.dt.bfloat16
I32, U32 = mybir.dt.int32, mybir.dt.uint32
ALU = mybir.AluOpType
ACT = mybir.ActivationFunctionType
AX = mybir.AxisListType

P = 128
B, S, D = 8, 256, 128
E, F = 8, 512
TOKENS = B * S
TT = TOKENS // P
FC = F // P
NX = TT - 1
NT = E + NX
HT = TT // 2
PARTS = ((0, 0, TT), (1, 0, HT), (1, HT, TT))
PER_BATCH = S // P
HEAD = 8
EPS = 1e-5
GROUPS = 4
GT = TT // GROUPS

ID, ROW, WIDE = D, D + 4, D + 4 + D
WIDTH = (ROW, WIDE)
NSCALE = 4096.0
WTOP = 2.0 ** 14
HSCALE = 2.0 ** -19
HUNIT = HSCALE * NSCALE

HALF = F // 2
W1H, W1L, W2H, W2L = (k * F for k in range(4))
B1, B2, BLOCK = 4 * HALF, 4 * HALF + FC, 4 * HALF + FC + D
STAGED = 2 * E * F // BLOCK
SPARED = 7 * TT * D // 2 // BLOCK
RING = STAGED + SPARED
XIN = 15
FIRST_ROWS = 9
YB = 10
AHEAD = 2


def build(nc, x_d, wq_d, bq_d, wk_d, bk_d, wv_d, bv_d, wg_d, bg_d, wo_d, bo_d,
          wr_d, br_d, w1_d, b1_d, w2_d, b2_d, out_d, sorted_d, y_d):
    ctx = ExitStack()
    with ctx:
        def sb(name, shape, dt=FP32):
            return ctx.enter_context(nc.sbuf_tensor(name, shape, dt))

        def ps(name, shape, dt=FP32):
            return ctx.enter_context(nc.psum_tensor(name, shape, dt))

        def sem(name):
            return ctx.enter_context(nc.semaphore(name))

        def fp16_view(t, n):
            return t[:].rearrange("p n w -> p (n w)").bitcast(FP16).rearrange("p (n w) -> p n w", n=n)

        norm = sb("norm", [P, TT, D])
        yin = sb("yin", [P, TT, D])
        rows = sb("rows", [P, TT, WIDE])
        xres = rows[:, :, ROW:WIDE]
        rows16 = fp16_view(rows, TT)
        stage = sb("stage", [P, 2 * E * F])
        spare = sb("spare", [P, 28 * S])
        w1 = stage[:, 0:E * F].rearrange("p (e f) -> p e f", e=E)
        w2 = stage[:, E * F:].rearrange("p (e f) -> p e f", e=E)
        ring = [stage[:, r * BLOCK:(r + 1) * BLOCK] for r in range(STAGED)] \
            + [spare[:, r * BLOCK:(r + 1) * BLOCK] for r in range(SPARED)]
        blocks = sb("blocks", [P, E, BLOCK])
        blocks16 = fp16_view(blocks, E)
        b1raw, b2raw = sb("b1raw", [E * FC, P]), sb("b2raw", [P, E, D])
        wa = sb("wa", [P, 4, D])
        wah, wal = sb("wah", [P, 4, D], FP16), sb("wal", [P, 4, D], FP16)
        wo, bqg, bkv, bob = sb("wo", [P, D]), sb("bqg", [P, 2]), sb("bkv", [P, 2, D]), sb("bob", [P, D])
        wrb, brb, wrsum = sb("wrb", [P, D]), sb("brb", [P, 1]), sb("wrsum", [P, 1])
        ident16, ident32 = sb("ident16", [P, P], FP16), sb("ident32", [P, P])
        before = sb("before", [P, P], BF16)
        ones16, ones32 = sb("ones16", [P, P], BF16), sb("ones32", [P, P])
        headmask = sb("headmask", [P, P])
        expert_no, first_slot = sb("expert_no", [P, E, TT]), sb("first_slot", [P, E, TT])
        extra_base = sb("extra_base", [P, E])
        extra_no = sb("extra_no", [P, NX, E])
        minus_half, minus_one = sb("minus_half", [P, TT]), sb("minus_one", [P, 1])
        empty_row = sb("empty_row", [P, WIDE])
        stats = [sb(f"stats{k}", [P, TT, 6]) for k in range(3)]
        mv = [sb(f"mv{k}", [P, TT, 2]) for k in range(3)]
        var, varh = [sb(f"var{k}", [P, TT]) for k in range(3)], [sb(f"varh{k}", [P, TT]) for k in range(3)]
        rs0, rsq = [sb(f"rs0{k}", [P, TT]) for k in range(3)], [sb(f"rsq{k}", [P, TT]) for k in range(3)]
        rstd, shift = [sb(f"rstd{k}", [P, TT]) for k in range(3)], [sb(f"shift{k}", [P, TT]) for k in range(3)]
        dots = sb("dots", [P, TT])
        key, rk, rki, rgt = sb("key", [P, TT]), sb("rk", [P, TT]), sb("rki", [P, TT], I32), sb("rgt", [P, TT])
        rfl, rex = sb("rfl", [P, TT], I32), sb("rex", [P, TT], I32)
        onehot = sb("onehot", [P, E * TT], BF16)
        tot, scan, pre, rank = sb("tot", [P, E * TT]), sb("scan", [P, E * TT]), sb("pre", [P, E * TT]), sb("rank", [P, E * TT])
        beyond, newer0, newer, slot0, slot1, slot2, slot3 = (
            sb(n, [P, E * TT]) for n in ("beyond", "newer0", "newer", "slot0", "slot1", "slot2", "slot3"))
        cnt, cnti, extra, extra_end = sb("cnt", [P, E]), sb("cnti", [P, E], I32), sb("extra", [P, E], I32), sb("extra_end", [P, E])
        adj0, adj, newer_from = sb("adj0", [P, E]), sb("adj", [P, E]), sb("newer_from", [P, E])
        cnt2, cnt3, rank_base0, rank_base, extra_end2 = (sb(n, [P, E]) for n in ("cnt2", "cnt3", "rank_base0", "rank_base", "extra_end2"))
        extra2 = sb("extra2", [P, E], I32)
        end0, added_end, adj21, adj20, adj2a, adj2 = (sb(n, [P, E]) for n in ("end0", "added_end", "adj21", "adj20", "adj2a", "adj2"))
        posf, pos = sb("posf", [P, TT]), sb("pos", [P, TT], I32)
        past, tef, te0, tef2 = sb("past", [P, NX, E]), sb("tef", [P, NX]), sb("te0", [P, NX]), sb("tef2", [P, NX])
        te = sb("te", [P, 2, NX], I32)
        wsum, wmax, wmaxt, wdiag = sb("wsum", [P, 2, E // 2]), sb("wmax", [P, 4]), sb("wmaxt", [4, 1]), sb("wdiag", [4, 4])
        gmax, sexp, sinv, sup = sb("gmax", [P, 4]), sb("sexp", [P, 4]), sb("sinv", [P, 4]), sb("sup", [P, 4])
        cy, ca, cg, s1h = sb("cy", [P, 1]), sb("ca", [P, 1]), sb("cg", [P, 1]), sb("s1h", [P, 1])
        xin = sb("xin", [P, XIN, WIDE])
        xin16 = fp16_view(xin, XIN)
        xt = sb("xt", [P, 3, 2, P], FP16)
        h32 = sb("h32", [P, 3, FC, P])
        hh, hl = sb("hh", [P, 3, FC, P], FP16), sb("hl", [P, 3, FC, P], FP16)
        ybuf = sb("ybuf", [P, YB, D])
        nh2, nl2 = sb("nh2", [P, 2, PER_BATCH, D], FP16), sb("nl2", [P, 2, PER_BATCH, D], FP16)
        nt_sb = sb("nt_sb", [P, 2, 2, S], FP16)
        pair = lambda k: spare[:, 2 * S * k:2 * S * (k + 1)].rearrange("p (b n) -> p b n", b=2)
        qe, qr, qm, qt, gt, gat = (pair(k) for k in range(6))
        ke, kk = (pair(k).rearrange("p b (t n) -> p b t n", t=PER_BATCH) for k in (6, 7))
        kv1 = spare[:, 16 * S:20 * S].rearrange("p (b t a n) -> p b t a n", b=2, t=PER_BATCH, a=2)
        x1bo = spare[:, 20 * S:28 * S].rearrange("p (t n) -> p t n", t=TT)
        kvm = sb("kvm", [P, 2, P])

        bank = [ps(f"bank{i}", [P, 512]) for i in range(8)]
        xt_ps = [bank[i][:, 0:P].bitcast(FP16).rearrange("p (a n) -> p a n", a=2) for i in (0, 1)]
        h_ps = [bank[i][:].rearrange("p (c n) -> p c n", c=FC) for i in (2, 3, 7)]
        y_ps = [bank[i][:, 0:D] for i in (4, 5)]
        r_ps = bank[6][:, 0:2 * E * TT].rearrange("p (a n) -> p a n", a=2)
        b1_ps, wmax_ps, gmax_ps = bank[7][:, 0:E * FC], bank[5][0:4, 0:P], bank[4][:, 0:4]
        nt_ps = bank[0][:, 0:S].bitcast(FP16).rearrange("p (a n) -> p a n", a=2)
        q_ps, g_ps = bank[1][:, 0:S], bank[7][:, 0:S]
        kv_ps = bank[2][:].rearrange("p (t a n) -> p t a n", t=PER_BATCH, a=2)
        kvh_ps = bank[3][:, 0:P]
        at_ps = bank[4][:, 0:S]
        o_ps = bank[5][:, 0:S].rearrange("p (t n) -> p t n", t=PER_BATCH)

        NORM1 = [(0, 2), (2, 2), (4, 4), (8, 4), (12, 4)]
        ROOTS = [(0, 0, TT)] + [(1, t, m) for t, m in NORM1] \
            + [(2, 0, HT), (2, HT, HT - PER_BATCH), (2, TT - PER_BATCH, PER_BATCH)]
        FIRST1, FIRST2 = 1, 1 + len(NORM1)
        norm1_of = lambda t: next(g for g, (t0, m) in enumerate(NORM1) if t0 <= t < t0 + m)
        TURNS = B + 2
        HALF_BATCHES = B // 2
        HALF_TURN = HALF_BATCHES + 2

        x_in = [sem(f"x_in{i}") for i in range(GROUPS)]
        y_in = [sem(f"y_in{i}") for i in range(len(NORM1))]
        route_in, b1_in, b2_in, w_in, wa_in = sem("route_in"), sem("b1_in"), sem("b2_in"), [[sem(f"w{i}_in{k}") for k in range(E // 2)] for i in (1, 2)], sem("wa_in")
        empty_set, filled = sem("empty_set"), [sem(f"filled{f}") for f in range(2)]
        consts_done, dve_step, pool_step = sem("consts_done"), sem("dve_step"), sem("pool_step")
        b1_turned, summed, wmax_ready, wmax_turned = sem("b1_turned"), sem("summed"), sem("wmax_ready"), sem("wmax_turned")
        wdiag_ready, wmax_spread, scales = sem("wdiag_ready"), sem("wmax_spread"), sem("scales")
        bias_ready, w_high, w_low, wa_ready = sem("bias_ready"), sem("w_high"), sem("w_low"), sem("wa_ready")
        var_ready, pow_ready, rstd_ready = sem("var_ready"), sem("pow_ready"), sem("rstd_ready")
        row_high, row_low = sem("row_high"), [sem(f"row_low{p}") for p in range(len(PARTS))]
        dispatched = [sem(f"dispatched{p}") for p in range(len(PARTS))]
        onehot_ready, ranked, routed = sem("onehot_ready"), sem("ranked"), sem("routed")
        L = [{n: sem(f"f{f}_{n}") for n in ("xt_done", "xt_copied", "h_done", "relu_done", "y_added",
                                            "hh_done", "hl_done", "y_done", "y_evac")}
             for f in range(2)]
        xin_ready = [sem(f"xin_ready{u}") for u in range(XIN)]
        block_ready = [sem(f"block_ready{u}") for u in range(RING)]
        stored = [sem(f"stored{u}") for u in range(YB)]
        x1_ready, x1bo_ready, normed = sem("x1_ready"), sem("x1bo_ready"), sem("normed")
        n2_high, n2_low, nt_done, nt_copied = sem("n2_high"), sem("n2_low"), sem("nt_done"), sem("nt_copied")
        q_done, g_done, kv_done = sem("q_done"), sem("g_done"), sem("kv_done")
        qe_ready, qm_ready, q_ready, g_ready = sem("qe_ready"), sem("qm_ready"), sem("q_ready"), sem("g_ready")
        kv1_ready, ke_ready, k_ready = sem("kv1_ready"), sem("ke_ready"), sem("k_ready")
        kvh_done, kvm_ready, at_done, gated_ready = sem("kvh_done"), sem("kvm_ready"), sem("at_done"), sem("gated_ready")
        o_done, x2_ready = sem("o_done"), sem("x2_ready")

        block = ctx.enter_context(nc.Block())

        x_v = x_d.rearrange("b (h p) d -> p (b h) d", p=P)
        out_v = out_d.rearrange("b (h p) d -> p (b h) d", p=P)
        group = lambda i: slice(GT * i, GT * i + GT)
        def tile_weights(t):
            if t < E:
                return blocks16[:, t], blocks[:, t]
            w = ring[(t - E) % RING]
            return w.bitcast(FP16), w

        def moved(f, k, total, places):
            return 16 * (f * len(range(k % places, total, places)) + k // places + 1)


        @block.sync
        def _(sp):
            for i in range(GROUPS):
                sp.dma_start(xres[:, group(i), :], x_v[:, group(i), :]).then_inc(x_in[i], 16)
                if i == 0:
                    sp.dma_start(wrb[:], wr_d.rearrange("(a n) -> a n", a=1).to_broadcast([P, D])).then_inc(route_in, 16)
                    sp.dma_start(brb[:], br_d.to_broadcast([P, 1])).then_inc(route_in, 16)
            sp.wait_ge(empty_set, 1)
            fill = lambda f: sp.dma_start(sorted_d[f].rearrange("(p k) w -> p k w", p=P),
                                          empty_row[:, 0:WIDTH[f]].rearrange("p (a w) -> p a w", a=1).to_broadcast(
                                              [P, NT, WIDTH[f]])
                                          ).then_inc(filled[f], 16)
            fill(0)
            sp.dma_start(b1raw[:], b1_d.rearrange("e (c p) -> (e c) p", p=P)).then_inc(b1_in, 16)
            for e in range(0, E, 2):
                sp.dma_start(w1[:, e:e + 2, :], w1_d[e:e + 2].rearrange("e p f -> p e f")).then_inc(w_in[0][e // 2], 16)
            for e in range(0, E, 2):
                sp.dma_start(w2[:, e:e + 2, :].rearrange("p e (c d) -> p e c d", c=FC),
                             w2_d[e:e + 2].rearrange("e (c p) d -> p e c d", p=P)).then_inc(w_in[1][e // 2], 16)
            for i, w in enumerate((wq_d, wg_d, wk_d, wv_d)):
                sp.dma_start(wa[:, i, :], w).then_inc(wa_in, 16)
            sp.dma_start(b2raw[:].rearrange("p e d -> p (e d)"),
                         b2_d.rearrange("(a e) d -> a (e d)", a=1).to_broadcast([P, E * D])).then_inc(b2_in, 16)
            sp.dma_start(wo[:], wo_d).then_inc(wa_in, 16)
            for i, b in enumerate((bq_d, bg_d)):
                sp.dma_start(bqg[:, i:i + 1], b.rearrange("(n a) -> n a", a=1)).then_inc(wa_in, 16)
            for i, b in enumerate((bk_d, bv_d)):
                sp.dma_start(bkv[:, i, :], b.rearrange("(a n) -> a n", a=1).to_broadcast([P, D])).then_inc(wa_in, 16)
            sp.dma_start(bob[:], bo_d.rearrange("(a n) -> a n", a=1).to_broadcast([P, D])).then_inc(wa_in, 16)

            def ffn_loads(f):
                s = L[f]

                def weights(x):
                    if x >= RING:
                        sp.wait_ge(s["y_evac"], E + x - RING + 1)
                    e = sp.value_load(te[0:1, f, x:x + 1], min_val=0, max_val=E - 1)
                    sp.dma_start(ring[x % RING], blocks[:, bass.ds(e, 1), :].rearrange("p a w -> p (a w)")
                                 ).then_inc(block_ready[x % RING], 16)

                def rows_in(t):
                    if t >= XIN:
                        sp.wait_ge(s["xt_done"], t - XIN + 1)
                        sp.wait_ge(stored[(t - XIN) % YB], moved(f, t - XIN, NT, YB))
                    sp.dma_start(xin[:, t % XIN, 0:WIDTH[f]], sorted_d[f][t * P:(t + 1) * P, :]).then_inc(xin_ready[t % XIN], 16)

                sp.wait_ge(routed, (1, 4)[f])
                early = 2 if f else 0
                for x in range(early):
                    weights(x)
                for p, (g, t0, t1) in enumerate(PARTS):
                    if g == f:
                        sp.wait_ge(dispatched[p], 16 * (t1 - t0))
                for t in range(FIRST_ROWS):
                    rows_in(t)
                if f == 0:
                    sp.wait_ge(w_low, E)
                late = iter(range(FIRST_ROWS, NT))
                for x in range(early, NX):
                    weights(x)
                    for t in islice(late, 2 if f == 1 and x >= NX // 2 else 1):
                        rows_in(t)
                for t in late:
                    rows_in(t)
                for t in range(NT - YB, NT):
                    sp.wait_ge(stored[t % YB], moved(f, t, NT, YB))

            ffn_loads(0)
            for i, (t, m) in enumerate(NORM1):
                sp.dma_start(yin[:, t:t + m, :], y_d.rearrange("(t p) d -> p t d", p=P)[:, t:t + m, :]
                             ).then_inc(y_in[i], 16)
            fill(1)
            ffn_loads(1)
        @block.gpsimd
        def _(pool):
            n = [0]
            G = nc.gpsimd

            def step(ins):
                n[0] += 1
                ins.then_inc(pool_step, 1)
                pool.wait_ge(pool_step, n[0])

            step(G.memset(empty_row[:], 0.0))
            G.memset(empty_row[:].bitcast(I32)[:, ID:ID + 1], TOKENS).then_inc(empty_set, 1)
            G.memset(minus_half[:], -0.5)
            G.memset(ident16[:], 0.0)
            G.memset(ident32[:], 0.0)
            G.memset(ones16[:], 1.0)
            G.memset(ones32[:], 1.0)
            G.memset(before[:], 0.0)
            G.memset(rows[:, :, ID + 1:ROW], 0.0)
            step(G.memset(headmask[:], 1.0))
            G.iota(rows[:].bitcast(I32)[:, :, ID:ID + 1], pattern=[[P, TT]], base=0, channel_multiplier=1)
            small = dict(channel_multiplier=0, allow_small_or_imprecise_dtypes=True)
            G.iota(expert_no[:], pattern=[[1, E], [0, TT]], base=0, **small)
            G.iota(first_slot[:], pattern=[[P, E], [0, TT]], base=0, **small)
            G.iota(extra_base[:], pattern=[[-P, E]], base=P * E - P, **small)
            G.iota(extra_no[:], pattern=[[1, NX], [0, E]], base=0, **small)
            for m in (ident16, ident32):
                G.affine_select(out=m[:], in_=m[:], compare_op=ALU.not_equal, fill=1.0, base=0,
                                pattern=[[-1, P]], channel_multiplier=1)
            G.affine_select(out=before[:], in_=before[:], compare_op=ALU.is_ge, fill=1.0, base=0,
                            pattern=[[-1, P]], channel_multiplier=1)
            hm = headmask[:].rearrange("p (g n) -> p g n", n=HEAD)
            step(G.affine_select(out=hm, in_=hm, compare_op=ALU.is_ge, fill=0.0, base=0,
                                 pattern=[[-HEAD, P // HEAD], [0, HEAD]], channel_multiplier=1))
            G.affine_select(out=hm, in_=hm, compare_op=ALU.is_ge, fill=0.0, base=HEAD - 1,
                            pattern=[[HEAD, P // HEAD], [0, HEAD]], channel_multiplier=-1).then_inc(consts_done, 1)

            def root(k):
                ln, t, m = ROOTS[k]
                pool.wait_ge(var_ready, k + 1)
                G.tensor_tensor(rs0[ln][:, t:t + m], var[ln][:, t:t + m], minus_half[:, t:t + m], ALU.pow
                                ).then_inc(pow_ready, 1)

            def row_lows(b):
                pool.wait_ge(row_high, B + b + 1)
                v = slice(PER_BATCH * b, PER_BATCH * (b + 1))
                G.tensor_tensor(rows16[:, v, D:2 * D], norm[:, v, :], rows16[:, v, 0:D],
                                ALU.subtract).then_inc(row_low[1], 1)

            def dispatch(p, first=0, last=TT):
                f, t0, t1 = PARTS[p]
                pool.wait_ge(filled[f], 16)
                pool.wait_ge(routed, p + 1)
                for j in range(t0 + first, min(t0 + last, t1)):
                    pool.wait_ge(row_low[p], (j - t0) // PER_BATCH + 1)
                    G.indirect_dma_start(
                        sorted_d[f], bass.IndirectOffsetOnAxis(ap=pos[:, j:j + 1].bitcast(U32), axis=0),
                        rows[:, j, 0:WIDTH[f]], None).then_inc(dispatched[p], 16)

            def collect(f, t):
                s, u = L[f], t % YB
                pool.wait_ge(s[("y_evac", "y_added")[f]], t + 1)
                G.indirect_dma_start(
                    (y_d, out_d.rearrange("b s d -> (b s) d"))[f],
                    bass.IndirectOffsetOnAxis(ap=xin[:, t % XIN, ID:ID + 1].bitcast(U32), axis=0),
                    ybuf[:, u, :], None, bounds_check=TOKENS - 1, oob_is_err=False).then_inc(stored[u], 16)

            def attention_lows(b):
                pool.wait_ge(n2_high, b + 1)
                if b >= 2:
                    pool.wait_ge(nt_done, b - 1)
                G.tensor_tensor(nl2[:, b % 2], norm[:, PER_BATCH * b:PER_BATCH * (b + 1), :], nh2[:, b % 2],
                                ALU.subtract).then_inc(n2_low, 1)

            root(0)
            dispatch(0)
            for t in range(NT):
                collect(0, t)
            for k in range(2):
                root(FIRST1 + k)
            attention_lows(0)
            root(FIRST1 + 2)
            attention_lows(1)
            for i in range(TURNS):
                if i == HALF_TURN:
                    root(FIRST2)
                if i < B:
                    k = i % 2
                    pool.wait_ge(qe_ready, i + 1)
                    G.tensor_scalar(qm[:, k], qe[:, k], 1.0, None, ALU.min).then_inc(qm_ready, 1)
                    pool.wait_ge(qm_ready, i + 1)
                    if i >= 2:
                        pool.wait_ge(at_done, i - 1)
                    G.tensor_tensor(qt[:, k], qm[:, k], qr[:, k], ALU.add).then_inc(q_ready, 1)
                if i == 0:
                    root(FIRST1 + 3)
                if i + 2 < B:
                    attention_lows(i + 2)
                if i == 2:
                    root(FIRST1 + 4)
                if i < B:
                    v = slice(PER_BATCH * i, PER_BATCH * (i + 1))
                    pool.wait_ge(x1_ready, norm1_of(PER_BATCH * i) + 1)
                    G.tensor_tensor(x1bo[:, v, :], xres[:, v, :],
                                    bob[:].rearrange("p (a n) -> p a n", a=1).to_broadcast([P, PER_BATCH, D]),
                                    ALU.add).then_inc(x1bo_ready, 1)
                if i == HALF_TURN + 2:
                    for b in range(B // 2):
                        row_lows(b)
            root(FIRST2 + 1)
            dispatch(1, 0, 1)
            root(FIRST2 + 2)
            dispatch(1, 1)
            dispatch(2)
            for t in range(NT):
                collect(1, t)

        @block.scalar
        def _(act):
            A = nc.scalar

            def normalise(ln, b, done):
                for j in range(PER_BATCH * b, PER_BATCH * (b + 1)):
                    ins = A.activation(norm[:, j, :], xres[:, j, :], ACT.Identity, bias=shift[ln][:, j:j + 1],
                                       scale=rstd[ln][:, j:j + 1])
                ins.then_inc(normed, 1)
                act.wait_ge(normed, done)

            def row_highs(f, b):
                normalise(2 * f, b, (2 * B if f else 0) + b + 1)
                v = slice(PER_BATCH * b, PER_BATCH * (b + 1))
                A.activation(rows16[:, v, 0:D], norm[:, v, :], ACT.Copy).then_inc(row_high, 1)

            def weight_sum(i, k):
                act.wait_ge(w_in[i][k], 16)
                n = 2 * F
                A.activation(h32[:].rearrange("p t c n -> p (t c n)")[:, 0:n],
                             (w1, w2)[i][:, 2 * k:2 * k + 2, :].rearrange("p e f -> p (e f)"), ACT.Abs,
                             accum_out=wsum[:, i, k:k + 1]).then_inc(summed, 1)
                act.wait_ge(summed, E // 2 * i + k + 1)

            def weight_highs(e):
                A.activation(blocks16[:, e:e + 2, W1H:W1H + F], w1[:, e:e + 2, :], ACT.Copy, scale=sup[:, 0:1])
                A.activation(blocks16[:, e:e + 2, W2H:W2H + F], w2[:, e:e + 2, :], ACT.Copy, scale=sup[:, 1:2]
                             ).then_inc(w_high, 2)

            weight_sum(0, 0)
            weight_sum(0, 1)
            act.wait_ge(rstd_ready, 1)
            for k, (i, c) in enumerate(((0, 2), (0, 3), (1, 0))):
                row_highs(0, k)
                weight_sum(i, c)
            for b in range(3, B):
                row_highs(0, b)
            act.wait_ge(scales, 1)
            for e in range(0, E, 2):
                weight_highs(e)
            A.activation(wah[:], wa[:], ACT.Copy, scale=sup[:, 2:3]).then_inc(w_high, 1)

            def ffn(f):
                s = L[f]

                def copy_turned(t):
                    act.wait_ge(s["xt_done"], t + 1)
                    if t >= 3:
                        act.wait_ge(s["h_done"], t - 2)
                    A.activation(xt[:, t % 3], xt_ps[t % 2], ACT.Copy).then_inc(s["xt_copied"], 1)

                def hidden(t):
                    act.wait_ge(s["h_done"], t + 1)
                    if t >= 3:
                        act.wait_ge(s["hl_done"], t - 2)
                    _, w = tile_weights(t)
                    for c in range(FC):
                        ins = A.activation(h32[:, t % 3, c, :], h_ps[t % 3][:, c, :], ACT.Relu,
                                           bias=w[:, B1 + c:B1 + c + 1], scale=HSCALE)
                    ins.then_inc(s["relu_done"], 1)

                if f == 0:
                    act.wait_ge(bias_ready, 1)
                copy_turned(0)
                for t in range(AHEAD):
                    copy_turned(t + 1)
                    hidden(t)
                for t in range(NT):
                    if t + AHEAD + 1 < NT:
                        copy_turned(t + AHEAD + 1)
                    if t + AHEAD < NT:
                        hidden(t + AHEAD)

            def attention_highs(b):
                act.wait_ge(rstd_ready, FIRST1 + 1 + norm1_of(PER_BATCH * b))
                normalise(1, b, B + b + 1)
                if b >= 2:
                    act.wait_ge(nt_done, b - 1)
                A.activation(nh2[:, b % 2], norm[:, PER_BATCH * b:PER_BATCH * (b + 1), :], ACT.Copy
                             ).then_inc(n2_high, 1)

            def copy_batch(b):
                act.wait_ge(nt_done, b + 1)
                if b >= 2:
                    act.wait_ge(kv_done, b - 1)
                    act.wait_ge(g_done, b - 1)
                A.activation(nt_sb[:, b % 2], nt_ps, ACT.Copy).then_inc(nt_copied, 1)

            ffn(0)
            attention_highs(0)
            copy_batch(0)
            attention_highs(1)
            for i in range(TURNS):
                k = i % 2
                if i < B:
                    act.wait_ge(q_done, i + 1)
                    if i >= 2:
                        act.wait_ge(q_ready, i - 1)
                    A.activation(qe[:, k], q_ps, ACT.Exp, bias=bqg[:, 0:1], scale=ca[:, 0:1])
                    A.activation(qr[:, k], q_ps, ACT.Relu, bias=bqg[:, 0:1], scale=ca[:, 0:1]).then_inc(qe_ready, 1)
                if i < B:
                    act.wait_ge(g_done, i + 1)
                    if i >= 2:
                        act.wait_ge(gated_ready, i - 1)
                    A.activation(gt[:, k], g_ps, ACT.Tanh, bias=bqg[:, 1:2], scale=cg[:, 0:1]).then_inc(g_ready, 1)
                if i + 1 < B:
                    copy_batch(i + 1)
                if i < B:
                    act.wait_ge(kv1_ready, i + 1)
                    if i >= 2:
                        act.wait_ge(k_ready, i - 1)
                    A.activation(ke[:, k], kv1[:, k, :, 0, :], ACT.Exp, bias=minus_one[:, 0:1]).then_inc(ke_ready, 1)
                if i + 2 < B:
                    attention_highs(i + 2)
                if i == HALF_TURN + 1:
                    act.wait_ge(rstd_ready, FIRST2 + 1)
                    row_highs(1, 0)
                if i == HALF_TURN + 2:
                    for b in range(1, B // 2):
                        row_highs(1, b)
            for b in range(B // 2, B):
                act.wait_ge(rstd_ready, FIRST2 + 2)
                row_highs(1, b)
            ffn(1)

        @block.tensor
        def _(pe):
            MM, T = nc.tensor.matmul, nc.tensor.transpose

            def split_matmul(out, whi, wlo, xhi, xlo):
                MM(out, whi, xhi, start=True, stop=False)
                MM(out, whi, xlo, start=False, stop=False)
                return MM(out, wlo, xhi, start=False, stop=True)

            def run_warm(n):
                for _ in range(n):
                    MM(bank[3][:], ident16[:], blocks16[:, 0, W1H:W1H + F], start=True, stop=True)

            def rank_tokens(p):
                pe.wait_ge(onehot_ready, p + 1)
                n = E * (PARTS[p][2] - PARTS[p][1])
                MM(r_ps[:, 1, 0:n], ones16[:], onehot[:, 0:n], start=True, stop=True)
                MM(r_ps[:, 0, 0:n], before[:], onehot[:, 0:n], start=True, stop=True).then_inc(ranked, 1)

            def ffn(f):
                s = L[f]

                def turn(t):
                    pe.wait_ge(xin_ready[t % XIN], moved(f, t, NT, XIN))
                    if t >= 2:
                        pe.wait_ge(s["xt_copied"], t - 1)
                    for a in range(2):
                        ins = T(xt_ps[t % 2][:, a, :], xin16[:, t % XIN, a * D:(a + 1) * D], ident16[:])
                    ins.then_inc(s["xt_done"], 1)

                def first(t):
                    w, _ = tile_weights(t)
                    pe.wait_ge(s["xt_copied"], t + 1)
                    if t >= 3:
                        pe.wait_ge(s["relu_done"], t - 2)
                    if t < E:
                        if f == 0:
                            pe.wait_ge(w_low, t + 1)
                    else:
                        x = t - E
                        pe.wait_ge(block_ready[x % RING], moved(f, x, NX, RING))
                    for c in range(FC):
                        hi, lo = (w[:, o + c * P:o + (c + 1) * P] for o in (W1H, W1L))
                        ins = split_matmul(h_ps[t % 3][:, c, :], hi, lo, xt[:, t % 3, 0, :], xt[:, t % 3, 1, :])
                    ins.then_inc(s["h_done"], 1)

                def second(t):
                    w, _ = tile_weights(t)
                    pe.wait_ge(s["hl_done"], t + 1)
                    if t >= 2:
                        pe.wait_ge(s["y_evac"], t - 1)
                    out = y_ps[t % 2]
                    for c in range(FC):
                        hi, lo = (w[:, o + c * D:o + (c + 1) * D] for o in (W2H, W2L))
                        MM(out, hh[:, t % 3, c, :], hi, start=(c == 0), stop=False)
                        MM(out, hh[:, t % 3, c, :], lo, start=False, stop=False)
                        ins = MM(out, hl[:, t % 3, c, :], hi, start=False, stop=(c == FC - 1))
                    ins.then_inc(s["y_done"], 1)

                turn(0)
                for t in range(AHEAD):
                    turn(t + 1)
                    first(t)
                for t in range(NT):
                    if t + AHEAD + 1 < NT:
                        turn(t + AHEAD + 1)
                    if t + AHEAD < NT:
                        first(t + AHEAD)
                    second(t)

            pe.wait_ge(consts_done, 1)
            rank_tokens(0)
            pe.wait_ge(b1_in, 16)
            T(b1_ps, b1raw[:], ident32[0:E * FC, 0:E * FC]).then_inc(b1_turned, 1)
            pe.wait_ge(wmax_ready, 1)
            T(wmax_ps, wmax[:], ident32[:]).then_inc(wmax_turned, 1)
            pe.wait_ge(wdiag_ready, 1)
            MM(gmax_ps, ones32[0:4, :], wdiag[:], start=True, stop=True).then_inc(wmax_spread, 1)
            ffn(0)

            def turn_batch(b):
                pe.wait_ge(n2_high, b + 1)
                pe.wait_ge(n2_low, b + 1)
                if b >= 1:
                    pe.wait_ge(nt_copied, b)
                for j in range(PER_BATCH):
                    for a, src in enumerate((nh2, nl2)):
                        ins = T(nt_ps[:, a, j * P:(j + 1) * P], src[:, b % 2, j, :], ident16[:])
                ins.then_inc(nt_done, 1)

            def project(b):
                k = b % 2
                pe.wait_ge(nt_copied, b + 1)
                if b >= 1:
                    pe.wait_ge(qe_ready, b)
                split_matmul(q_ps, wah[:, 0, :], wal[:, 0, :], nt_sb[:, k, 0, :], nt_sb[:, k, 1, :]).then_inc(q_done, 1)
                if b >= 1:
                    pe.wait_ge(kv1_ready, b)
                kvh, kvl = (w[:, 2:4, :].rearrange("p a n -> p (a n)") for w in (wah, wal))
                for j in range(PER_BATCH):
                    out = kv_ps[:, j].rearrange("p a n -> p (a n)")
                    th, tl = (nt_sb[:, k, a, j * P:(j + 1) * P] for a in range(2))
                    MM(out, th, kvh, start=True, stop=False)
                    MM(out, th, kvl, start=False, stop=False)
                    ins = MM(out, tl, kvh, start=False, stop=True)
                ins.then_inc(kv_done, 1)
                if b >= 1:
                    pe.wait_ge(g_ready, b)
                split_matmul(g_ps, wah[:, 1, :], wal[:, 1, :], nt_sb[:, k, 0, :], nt_sb[:, k, 1, :]).then_inc(g_done, 1)

            def keys_values(b):
                k = b % 2
                pe.wait_ge(k_ready, b + 1)
                if b >= 1:
                    pe.wait_ge(kvm_ready, b)
                for j in range(PER_BATCH):
                    ins = MM(kvh_ps, kk[:, k, j, :], kv1[:, k, j, 1, :], start=(j == 0), stop=(j == PER_BATCH - 1))
                ins.then_inc(kvh_done, 1)

            def attend(b):
                k = b % 2
                pe.wait_ge(kvm_ready, b + 1)
                pe.wait_ge(q_ready, b + 1)
                if b >= 1:
                    pe.wait_ge(gated_ready, b)
                MM(at_ps, kvm[:, k], qt[:, k], start=True, stop=True).then_inc(at_done, 1)

            def project_out(b):
                k = b % 2
                pe.wait_ge(gated_ready, b + 1)
                if b >= 1:
                    pe.wait_ge(x2_ready, b)
                for j in range(PER_BATCH):
                    ins = MM(o_ps[:, j, :], gat[:, k, j * P:(j + 1) * P], wo[:], start=True, stop=True)
                ins.then_inc(o_done, 1)

            pe.wait_ge(x1_ready, 1)
            run_warm(12)
            turn_batch(0)
            pe.wait_ge(wa_ready, 1)
            for i in range(TURNS):
                if i < B:
                    project(i)
                if i + 1 < B:
                    turn_batch(i + 1)
                if 0 <= i - 1 < B:
                    keys_values(i - 1)
                if i == HALF_TURN + 2:
                    rank_tokens(1)
                if 0 <= i - 2 < B:
                    project_out(i - 2)
                if 0 <= i - 1 < B:
                    attend(i - 1)
            rank_tokens(2)
            ffn(1)

        @block.vector
        def _(dve):
            n = [0]
            V = nc.vector

            def step(ins):
                n[0] += 1
                ins.then_inc(dve_step, 1)
                dve.wait_ge(dve_step, n[0])

            def signal(ins):
                n[0] += 1
                ins.then_inc(dve_step, 1)
                return n[0]

            def tile_stats(ln, t, m):
                for j in range(t, t + m):
                    ins = V.bn_stats(stats[ln][:, j, :], xres[:, j, :])
                return ins

            def tile_dots(t, m):
                for j in range(t, t + m):
                    ins = V.tensor_tensor_reduce(out=norm[:, j, :], in0=xres[:, j, :], in1=wrb[:], scale=1.0,
                                                 scalar=0.0, op0=ALU.mult, op1=ALU.add, accum_out=dots[:, j:j + 1])
                return ins

            def aggregate(ln, t, m):
                for j in range(t, t + m):
                    ins = V.bn_aggr(mv[ln][:, j, :], stats[ln][:, j, :])
                return ins

            def add_eps(ln, t, m):
                V.tensor_scalar(var[ln][:, t:t + m], mv[ln][:, t:t + m, 1], EPS, None, ALU.add).then_inc(var_ready, 1)
                V.tensor_scalar(varh[ln][:, t:t + m], mv[ln][:, t:t + m, 1], EPS, -0.5 * NSCALE, ALU.add, ALU.mult)

            def variance(ln, t, m):
                step(aggregate(ln, t, m))
                add_eps(ln, t, m)

            def inverse_root_levels(k, pieces=1):
                ln, t, _ = ROOTS[k]
                v = slice(t, t + sum(m for _, _, m in ROOTS[k:k + pieces]))
                dve.wait_ge(pow_ready, k + pieces)
                n = signal(V.tensor_tensor(rsq[ln][:, v], rs0[ln][:, v], rs0[ln][:, v], ALU.mult))
                yield
                dve.wait_ge(dve_step, n)
                n = signal(V.tensor_tensor(varh[ln][:, v], rsq[ln][:, v], varh[ln][:, v], ALU.mult))
                yield
                dve.wait_ge(dve_step, n)
                n = signal(V.scalar_tensor_tensor(rstd[ln][:, v], varh[ln][:, v], 1.5 * NSCALE, rs0[ln][:, v], ALU.add, ALU.mult))
                yield
                dve.wait_ge(dve_step, n)
                V.scalar_tensor_tensor(shift[ln][:, v], mv[ln][:, v, 0], -1.0, rstd[ln][:, v], ALU.mult, ALU.mult
                                       ).then_inc(rstd_ready, 1)
                yield

            def inverse_root(k, pieces=1):
                for _ in inverse_root_levels(k, pieces):
                    pass

            absmax = lambda out, a: V.tensor_reduce(out, a, AX.X, ALU.max, apply_absolute_value=True)

            def row_lows(f, b):
                dve.wait_ge(row_high, B * f + b + 1)
                v = slice(PER_BATCH * b, PER_BATCH * (b + 1))
                V.tensor_tensor(rows16[:, v, D:2 * D], norm[:, v, :], rows16[:, v, 0:D], ALU.subtract
                                ).then_inc(row_low[2 * f], 1)

            def by_expert(a, p):
                m = PARTS[p][2] - PARTS[p][1]
                return a[:, 0:E * m].rearrange("p (e t) -> p e t", e=E)

            def spread(a, p):
                return a.rearrange("p (e o) -> p e o", o=1).to_broadcast([P, E, PARTS[p][2] - PARTS[p][1]])

            def raw_key(p):
                f, t0, t1 = PARTS[p]
                v = slice(t0, t1)
                return V.scalar_tensor_tensor(key[:, v], mv[2 * f][:, v, 0], wrsum[:, 0:1], dots[:, v], ALU.mult, ALU.subtract)

            def route_experts(p):
                f, t0, t1 = PARTS[p]
                v, m = slice(t0, t1), t1 - t0
                n = signal(V.tensor_tensor(rgt[:, v], key[:, v], rstd[2 * f][:, v], ALU.mult))
                yield
                dve.wait_ge(dve_step, n)
                V.tensor_scalar(rki[:, v], rgt[:, v], -1.0 / NSCALE, brb[:, 0:1], ALU.mult, ALU.add)
                n = signal(V.tensor_scalar(rk[:, v], rgt[:, v], -1.0 / NSCALE, brb[:, 0:1], ALU.mult, ALU.add))
                yield
                dve.wait_ge(dve_step, n)
                n = signal(V.tensor_tensor(rgt[:, v], rki[:, v], rk[:, v], ALU.is_gt))
                yield
                dve.wait_ge(dve_step, n)
                n = signal(V.tensor_tensor(rfl[:, v], rki[:, v], rgt[:, v], ALU.subtract))
                yield
                dve.wait_ge(dve_step, n)
                n = signal(V.tensor_scalar(rex[:, v], rfl[:, v], E - 1, None, ALU.bitwise_and))
                yield
                dve.wait_ge(dve_step, n)
                V.tensor_tensor(by_expert(onehot, p), rex[:, v].rearrange("p (a t) -> p a t", a=1).to_broadcast([P, E, m]),
                                expert_no[:, :, 0:m], ALU.is_equal).then_inc(onehot_ready, 1)
                yield

            def route_first(p):
                f, t0, t1 = PARTS[p]
                n, m = E * (t1 - t0), t1 - t0
                dve.wait_ge(ranked, p + 1)
                V.tensor_tensor_scan(scan[:, 0:n], ones32[:, 0:n], r_ps[:, 1, 0:n], 0.0, ALU.mult, ALU.add)
                V.tensor_copy(tot[:, 0:n], r_ps[:, 1, 0:n])
                k = signal(V.tensor_reduce(cnt[:], by_expert(r_ps[:, 1], p), AX.X, ALU.add))
                yield
                dve.wait_ge(dve_step, k)
                V.tensor_tensor(pre[:, 0:n], scan[:, 0:n], tot[:, 0:n], ALU.subtract)
                k = signal(V.tensor_scalar(cnti[:], cnt[:], float(P), -1.0, ALU.max, ALU.add))
                yield
                dve.wait_ge(dve_step, k)
                V.tensor_tensor(by_expert(rank, p), by_expert(pre, p), by_expert(pre, p)[:, :, 0:1].to_broadcast([P, E, m]),
                                ALU.subtract)
                k = signal(V.tensor_scalar(extra[:], cnti[:], 7, None, ALU.logical_shift_right))
                yield
                dve.wait_ge(dve_step, k)
                V.tensor_tensor(rank[:, 0:n], rank[:, 0:n], r_ps[:, 0, 0:n], ALU.add)
                k = signal(V.tensor_tensor_scan(extra_end[:], ones32[:, 0:E], extra[:], 0.0, ALU.mult, ALU.add))
                yield
                dve.wait_ge(dve_step, k)
                V.tensor_tensor(by_expert(slot0, p), by_expert(rank, p), first_slot[:, :, 0:m], ALU.add)
                V.tensor_tensor(past[:], extra_no[:], extra_end[:].rearrange("p (a e) -> p a e", a=1).to_broadcast([P, NX, E]),
                                ALU.is_ge)
                k = signal(V.tensor_tensor(adj0[:], extra_end[:], extra[:], ALU.subtract))
                yield
                dve.wait_ge(dve_step, k)
                k = signal(V.scalar_tensor_tensor(adj[:], adj0[:], float(P), extra_base[:], ALU.mult, ALU.add))
                yield
                dve.wait_ge(dve_step, k)
                k = signal(V.scalar_tensor_tensor(by_expert(beyond, p), by_expert(rank, p), float(P), spread(adj[:], p),
                                                  ALU.is_ge, ALU.mult))
                yield
                dve.wait_ge(dve_step, k)
                V.tensor_reduce(tef[:], past[:], AX.X, ALU.add)
                k = signal(V.tensor_tensor(slot1[:, 0:n], slot0[:, 0:n], beyond[:, 0:n], ALU.add))
                yield
                dve.wait_ge(dve_step, k)
                k = signal(V.tensor_tensor(slot3[:, 0:n], slot1[:, 0:n], onehot[:, 0:n], ALU.mult))
                if p == 0:
                    V.tensor_scalar(te[:, f], tef[:], float(E - 1), None, ALU.min)
                yield
                dve.wait_ge(dve_step, k)
                k = signal(V.tensor_reduce(posf[:, 0:m], by_expert(slot3, p).rearrange("p e t -> p t e"), AX.X, ALU.add))
                yield
                dve.wait_ge(dve_step, k)
                V.tensor_copy(pos[:, t0:t1], posf[:, 0:m]).then_inc(routed, 1)
                yield

            def second_bases():
                V.tensor_scalar(newer_from[:], extra[:], float(P), float(P), ALU.mult, ALU.add)
                step(V.tensor_scalar(end0[:], extra_end[:], -1.0, extra_end[:, E - 1:E], ALU.mult, ALU.add))
                V.scalar_tensor_tensor(te0[:], past[:, :, E - 1], -float(E), tef[:], ALU.mult, ALU.add)
                step(V.tensor_tensor(adj21[:], end0[:], adj0[:], ALU.subtract))
                V.tensor_scalar(adj20[:], adj21[:], float(P), None, ALU.mult)

            def route_second(p):
                f, t0, t1 = PARTS[p]
                n, m = E * (t1 - t0), t1 - t0
                dve.wait_ge(ranked, p + 1)
                V.tensor_tensor_scan(scan[:, 0:n], ones32[:, 0:n], r_ps[:, 1, 0:n], 0.0, ALU.mult, ALU.add)
                V.tensor_copy(tot[:, 0:n], r_ps[:, 1, 0:n])
                step(V.tensor_reduce(cnt2[:], by_expert(r_ps[:, 1], p), AX.X, ALU.add))
                V.tensor_tensor(rank_base0[:], cnt[:], by_expert(tot, p)[:, :, 0], ALU.add)
                V.tensor_tensor(slot1[:, 0:n], scan[:, 0:n], tot[:, 0:n], ALU.subtract)
                step(V.tensor_tensor(cnt3[:], cnt2[:], cnt[:], ALU.add))
                V.tensor_tensor(rank_base[:], by_expert(scan, p)[:, :, 0], rank_base0[:], ALU.subtract)
                V.tensor_tensor(rank[:, 0:n], slot1[:, 0:n], r_ps[:, 0, 0:n], ALU.add)
                step(V.tensor_scalar(cnti[:], cnt3[:], float(P), -1.0, ALU.max, ALU.add))
                V.tensor_tensor(by_expert(rank, p), by_expert(rank, p), spread(rank_base[:], p), ALU.subtract)
                step(V.tensor_scalar(extra2[:], cnti[:], 7, None, ALU.logical_shift_right))
                V.scalar_tensor_tensor(by_expert(beyond, p), by_expert(rank, p), float(P), spread(adj[:], p), ALU.is_ge, ALU.mult)
                step(V.tensor_tensor_scan(extra_end2[:], ones32[:, 0:E], extra2[:], 0.0, ALU.mult, ALU.add))
                V.tensor_tensor(by_expert(newer0, p), by_expert(rank, p), spread(newer_from[:], p), ALU.is_ge)
                step(V.tensor_tensor(adj2a[:], extra_end2[:], extra2[:], ALU.subtract))
                V.tensor_tensor(by_expert(slot0, p), by_expert(rank, p), first_slot[:, :, 0:m], ALU.add)
                step(V.scalar_tensor_tensor(adj2[:], adj2a[:], float(P), adj20[:], ALU.mult, ALU.add))
                V.tensor_tensor(slot1[:, 0:n], slot0[:, 0:n], beyond[:, 0:n], ALU.add)
                step(V.tensor_tensor(by_expert(newer, p), by_expert(newer0, p), spread(adj2[:], p), ALU.mult))
                step(V.tensor_tensor(slot2[:, 0:n], slot1[:, 0:n], newer[:, 0:n], ALU.add))
                V.tensor_tensor(added_end[:], extra_end2[:], end0[:], ALU.add)
                step(V.tensor_tensor(slot3[:, 0:n], slot2[:, 0:n], onehot[:, 0:n], ALU.mult))
                step(V.tensor_reduce(posf[:, 0:m], by_expert(slot3, p).rearrange("p e t -> p t e"), AX.X, ALU.add))
                V.tensor_copy(pos[:, t0:t1], posf[:, 0:m]).then_inc(routed, 1)
                for b in range(B // 2, B):
                    row_lows(1, b)
                step(V.tensor_tensor(past[:], extra_no[:], added_end[:].rearrange("p (a e) -> p a e", a=1).to_broadcast([P, NX, E]),
                                     ALU.is_ge))
                step(V.tensor_reduce(tef[:], past[:], AX.X, ALU.add))
                step(V.tensor_tensor(tef2[:], tef[:], te0[:], ALU.add))
                V.tensor_scalar(te[:, f], tef2[:], float(E - 1), None, ALU.min).then_inc(routed, 1)

            def run(levels):
                for _ in levels:
                    pass

            def first_half_routing():
                yield from inverse_root_levels(FIRST2)
                dve.wait_ge(rstd_ready, FIRST2 + 1)
                yield from route_experts(1)
                yield from route_first(1)

            def weight_lows(e):
                dve.wait_ge(w_high, e + 2)
                for w, hi, lo, g in ((w1, W1H, W1L, 0), (w2, W2H, W2L, 1)):
                    ins = V.scalar_tensor_tensor(blocks16[:, e:e + 2, lo:lo + F], w[:, e:e + 2, :], sup[:, g:g + 1],
                                                 blocks16[:, e:e + 2, hi:hi + F], ALU.mult, ALU.subtract)
                ins.then_inc(w_low, 2)

            def attention_weights():
                dve.wait_ge(w_high, E + 1)
                V.scalar_tensor_tensor(wal[:], wa[:], sup[:, 2:3], wah[:], ALU.mult, ALU.subtract)
                V.tensor_scalar(ca[:], sexp[:, 2:3], 1.0 / (NSCALE * WTOP), None, ALU.mult)
                V.tensor_scalar(cg[:], sexp[:, 2:3], 0.5 / (NSCALE * WTOP), None, ALU.mult)
                V.tensor_scalar(wo[:], wo[:], 0.5, None, ALU.mult)
                V.tensor_scalar(bqg[:, 1:2], bqg[:, 1:2], 0.5, None, ALU.mult)
                V.memset(minus_one[:], -1.0)
                V.tensor_scalar(bkv[:, 0, :], bkv[:, 0, :], 1.0, None, ALU.add).then_inc(wa_ready, 1)

            def input_levels(g):
                t, m = NORM1[g]
                dve.wait_ge(y_in[g], 16)
                V.tensor_tensor(xres[:, t:t + m, :], xres[:, t:t + m, :], yin[:, t:t + m, :], ALU.add
                                ).then_inc(x1_ready, 1)
                yield
                dve.wait_ge(x1_ready, g + 1)
                tile_stats(1, t, m // 2)
                yield
                n = signal(tile_stats(1, t + m // 2, m // 2))
                yield
                dve.wait_ge(dve_step, n)
                n = signal(aggregate(1, t, m))
                yield
                dve.wait_ge(dve_step, n)
                add_eps(1, t, m)
                yield

            def ffn(f):
                s = L[f]

                def hidden_high(t):
                    k = t % 3
                    dve.wait_ge(s["relu_done"], t + 1)
                    if t >= 3:
                        dve.wait_ge(s["y_done"], t - 2)
                    V.tensor_copy(hh[:, k], h32[:, k]).then_inc(s["hh_done"], 1)

                def split_hidden(t):
                    hidden_high(t)
                    hidden_low(t)

                def hidden_low(t):
                    k = t % 3
                    dve.wait_ge(s["hh_done"], t + 1)
                    V.tensor_tensor(hl[:, k], h32[:, k], hh[:, k], ALU.subtract).then_inc(s["hl_done"], 1)

                def output(t):
                    u = t % YB
                    dve.wait_ge(s["y_done"], t + 1)
                    if t >= YB:
                        dve.wait_ge(stored[u], moved(f, t - YB, NT, YB))
                    _, w = tile_weights(t)
                    V.scalar_tensor_tensor(ybuf[:, u, :], y_ps[t % 2], cy[:, 0:1], w[:, B2:B2 + D],
                                           ALU.mult, ALU.add).then_inc(s["y_evac"], 1)

                def add_x2(t):
                    dve.wait_ge(s["y_evac"], t + 1)
                    dve.wait_ge(xin_ready[t % XIN], moved(f, t, NT, XIN))
                    V.tensor_tensor(ybuf[:, t % YB, :], ybuf[:, t % YB, :], xin[:, t % XIN, ROW:WIDE], ALU.add
                                    ).then_inc(s["y_added"], 1)

                for t in range(AHEAD):
                    split_hidden(t)
                for t in range(NT):
                    if t >= 1:
                        output(t - 1)
                    if t + AHEAD < NT:
                        hidden_high(t + AHEAD)
                    if f == 1 and t >= 1:
                        add_x2(t - 1)
                    if t + AHEAD < NT:
                        hidden_low(t + AHEAD)
                output(NT - 1)
                if f == 1:
                    add_x2(NT - 1)

            for i in range(GROUPS):
                dve.wait_ge(x_in[i], 16)
                ins = tile_stats(0, GT * i, GT)
            step(ins)
            variance(0, 0, TT)
            dve.wait_ge(route_in, 32)
            V.tensor_reduce(wrsum[:], wrb[:], AX.X, ALU.add)
            step(tile_dots(0, TT))
            raw_key(0)
            inverse_root(0)
            dve.wait_ge(rstd_ready, 1)
            dve.wait_ge(consts_done, 1)
            run(route_experts(0))
            run(route_first(0))
            for b in range(B - 2):
                row_lows(0, b)
                if b in (2, 3, 4):
                    dve.wait_ge(w_in[1][b - 1], 16)
                    absmax(wsum[:, 1, b - 1:b], w2[:, 2 * (b - 1):2 * b, :].rearrange("p e f -> p (e f)"))

            dve.wait_ge(b1_turned, 1)
            absmax(wmax[:, 3:4], b1_ps)
            dve.wait_ge(wa_in, 16 * 10)
            dve.wait_ge(summed, E // 2 + 1)
            step(absmax(wmax[:, 2:3], wa[:].rearrange("p e d -> p (e d)")))
            step(absmax(wmax[:, 0:2], wsum[:]))
            V.tensor_tensor(wmax[:, 0:1], wmax[:, 0:1], wmax[:, 3:4], ALU.max).then_inc(wmax_ready, 1)
            dve.wait_ge(wmax_turned, 1)
            step(V.tensor_reduce(wmaxt[:], wmax_ps, AX.X, ALU.max))
            V.tensor_scalar(wdiag[:], ident32[0:4, 0:4], wmaxt[:, 0:1], None, ALU.mult).then_inc(wdiag_ready, 1)
            dve.wait_ge(wmax_spread, 1)
            step(V.tensor_scalar(gmax[:], gmax_ps, 1e-30, None, ALU.max))
            step(V.tensor_scalar(sexp[:].bitcast(I32), gmax[:].bitcast(I32), 0x7F800000, None, ALU.bitwise_and))
            step(V.tensor_scalar(sinv[:].bitcast(I32), sexp[:].bitcast(I32), -1.0, float(254 << 23), ALU.mult, ALU.add))
            V.tensor_scalar(sup[:], sinv[:], WTOP, None, ALU.mult).then_inc(scales, 1)
            row_lows(0, B - 2)
            row_lows(0, B - 1)
            step(V.tensor_scalar(s1h[:], sinv[:, 0:1], WTOP * HUNIT, None, ALU.mult))
            V.tensor_scalar(blocks[:, :, B1:B1 + FC], b1_ps.rearrange("p (e c) -> p e c", e=E), s1h[:, 0:1], None, ALU.mult)
            V.tensor_scalar(cy[:], sexp[:, 0:1], sexp[:, 1:2], None, ALU.mult)
            dve.wait_ge(b2_in, 16)
            step(V.tensor_scalar(blocks[:, :, B2:B2 + D], b2raw[:], 0.5, None, ALU.mult))
            V.tensor_scalar(cy[:], cy[:], 0.5 / (HUNIT * WTOP * WTOP), None, ALU.mult).then_inc(bias_ready, 1)
            for e in range(0, E, 2):
                weight_lows(e)
            attention_weights()

            ffn(0)

            bkv2 = bkv[:].rearrange("p a n -> p (a n)")
            dve.wait_ge(wa_ready, 1)
            run(input_levels(0))
            run(input_levels(1))
            inverse_root(FIRST1)
            run(input_levels(2))
            inverse_root(FIRST1 + 1)
            run(input_levels(3))
            SIDE = {0: inverse_root_levels(FIRST1 + 2), 1: chain(inverse_root_levels(FIRST1 + 3), input_levels(4)),
                    3: inverse_root_levels(FIRST1 + 4)}
            side = iter(())
            for i in range(TURNS):
                b, c, d = i - 1, i - 2, i - 3
                if i == 0:
                    next(SIDE[0], None)
                if 0 <= d < B - 2:
                    if d >= 1 and d != HALF_BATCHES:
                        dve.wait_ge(dve_step, stats_of)
                        aggregate(2, PER_BATCH * (d - 1), PER_BATCH)
                    dve.wait_ge(x2_ready, d + 1)
                    stats_of = signal(tile_stats(2, PER_BATCH * d, PER_BATCH))
                    ins = tile_dots(PER_BATCH * d, PER_BATCH)
                    if i == HALF_TURN:
                        dve.wait_ge(dve_step, stats_of)
                        step(aggregate(2, PER_BATCH * d, PER_BATCH))
                        add_eps(2, 0, HT)
                        raw_key(1)
                if i < B:
                    k = i % 2
                    dve.wait_ge(kv_done, i + 1)
                    if i >= 2:
                        dve.wait_ge(kvh_done, i - 1)
                    for j in range(PER_BATCH):
                        ins = V.scalar_tensor_tensor(kv1[:, k, j].rearrange("p a n -> p (a n)"),
                                                     kv_ps[:, j].rearrange("p a n -> p (a n)"), ca[:, 0:1], bkv2,
                                                     ALU.mult, ALU.add)
                    ins.then_inc(kv1_ready, 1)
                side = SIDE.get(i, side)
                if i < TURNS - 1:
                    next(side, None)
                if 0 <= b < B:
                    k = b % 2
                    dve.wait_ge(kvh_done, b + 1)
                    if b >= 2:
                        dve.wait_ge(at_done, b - 1)
                    V.tensor_tensor(kvm[:, k], kvh_ps, headmask[:], ALU.mult).then_inc(kvm_ready, 1)
                for _ in range(4 if i == TURNS - 2 else 1 if i < TURNS - 2 else 0):
                    next(side, None)
                if 0 <= c < B:
                    v = slice(PER_BATCH * c, PER_BATCH * (c + 1))
                    dve.wait_ge(o_done, c + 1)
                    dve.wait_ge(x1bo_ready, c + 1)
                    V.tensor_tensor(xres[:, v, :], o_ps, x1bo[:, v, :], ALU.add).then_inc(x2_ready, 1)
                if i == HALF_TURN:
                    side = first_half_routing()
                next(side, None)
                if i < B:
                    k = i % 2
                    dve.wait_ge(ke_ready, i + 1)
                    V.scalar_tensor_tensor(kk[:, k], ke[:, k], 1.0, kv1[:, k, :, 0, :], ALU.min, ALU.max
                                           ).then_inc(k_ready, 1)
                next(side, None)
                if 0 <= b < B:
                    k = b % 2
                    dve.wait_ge(at_done, b + 1)
                    dve.wait_ge(g_ready, b + 1)
                    if b >= 2:
                        dve.wait_ge(o_done, b - 1)
                    V.scalar_tensor_tensor(gat[:, k], gt[:, k], 1.0, at_ps, ALU.add, ALU.mult).then_inc(gated_ready, 1)
                if i == TURNS - 2:
                    dve.wait_ge(dve_step, stats_of)
                    dve.wait_ge(x2_ready, B - 1)
                    aggregate(2, PER_BATCH * d, PER_BATCH)
                    stats_of = signal(tile_stats(2, PER_BATCH * (d + 1), PER_BATCH))
                    next(side, None)
                    dve.wait_ge(dve_step, stats_of)
                    aggregate_of = signal(aggregate(2, PER_BATCH * (d + 1), PER_BATCH))
                    next(side, None)
                    dve.wait_ge(dve_step, aggregate_of)
                    add_eps(2, HT, HT - PER_BATCH)
                    next(side, None)
                if i == 2:
                    run(side)
                next(side, None)
            run(side)
            dve.wait_ge(x2_ready, B)
            step(tile_stats(2, TT - PER_BATCH, PER_BATCH))
            variance(2, TT - PER_BATCH, PER_BATCH)
            tile_dots(TT - 2 * PER_BATCH, 2 * PER_BATCH)
            second_bases()
            raw_key(2)
            inverse_root(FIRST2 + 1, pieces=2)
            dve.wait_ge(rstd_ready, FIRST2 + 2)
            run(route_experts(2))
            route_second(2)
            ffn(1)
    return nc


_INS = ["L0_attn_x", "L0_attn_Wq", "L0_attn_bq", "L0_attn_Wk", "L0_attn_bk", "L0_attn_Wv", "L0_attn_bv",
        "L0_attn_Wg", "L0_attn_bg", "L0_attn_Wo", "L0_attn_bo", "L0_ffn_wr", "L0_ffn_br", "L0_ffn_W1",
        "L0_ffn_b1", "L0_ffn_W2", "L0_ffn_b2"]


def kernel(**inputs):
    import concourse.bacc as bacc
    from concourse.bass_utils import run_bass_kernel_spmd

    nc = bacc.Bacc("TRN2", target_bir_lowering=False, num_devices=1)
    arrays, args = {}, []
    for name in _INS:
        a = np.ascontiguousarray(inputs[name])
        if a.ndim == 0:
            a = a.reshape(1, 1)
        arrays[f"in_{name}"] = a
        args.append(nc.dram_tensor(f"in_{name}", a.shape, mybir.dt.from_np(a.dtype), kind="ExternalInput").ap())
    out = nc.dram_tensor("out", (B, S, D), FP32, kind="ExternalOutput").ap()
    sorted_rows = [nc.dram_tensor(f"sorted{f}", (NT * P, WIDTH[f]), FP32, kind="Internal").ap() for f in range(2)]
    y = nc.dram_tensor("y", (TOKENS, D), FP32, kind="Internal").ap()
    build(nc, *args, out, sorted_rows, y)
    r = run_bass_kernel_spmd(nc, [arrays], core_ids=[0])
    return r.results[0]["out"]
```
